# Optimizing a Trainium2 kernel written in Bass

```python
import numpy as np
import jax
import jax.numpy as jnp

def _softmax(x, axis=-1):
    return jax.nn.softmax(x, axis=axis)

def _gelu(x):
    return jax.nn.gelu(x, approximate=True)

def _silu(x):
    return jax.nn.silu(x)

def _sigmoid(x):
    return jax.nn.sigmoid(x)

def _layernorm(x, axis=-1, eps=1e-05):
    m = jnp.mean(x, axis=axis, keepdims=True)
    v = jnp.var(x, axis=axis, keepdims=True)
    return (x - m) / jnp.sqrt(v + eps)

def _scatter_add(tgt, idx, src, axis=0):
    return tgt.at[idx].add(src)

def _segment_sum(src, seg, n):
    return jax.ops.segment_sum(src, seg, n)
kernel_name = 'mk_seq_preln_d1_jaxref_r2_f092b4'

def setup_inputs(seed: int=0):
    np.random.seed(seed)
    _w = jnp.asarray

    def _L0_attn_setup():
        import jax, jax.numpy as jnp
        import numpy as np
        import math
        B, L, D, N = (8, 2048, 512, 16)
        key = jax.random.key(seed)
        k1, k2, k3, k4, k5, k6 = jax.random.split(key, 6)
        return {'x': jax.random.normal(k1, (B, L, D), dtype=jnp.float32), 'delta': jax.random.normal(k2, (D, N, 1), dtype=jnp.float32), 'alpha': jax.random.normal(k3, (D, N, 1), dtype=jnp.float32), 'beta': jax.random.normal(k4, (D, N, 1), dtype=jnp.float32), 'gamma': jax.random.normal(k5, (D, N), dtype=jnp.float32), 'omega': jax.random.normal(k6, (D,), dtype=jnp.float32)}
    _L0_attn_in = _L0_attn_setup()

    def _L0_ffn_setup():
        import jax, jax.numpy as jnp
        import numpy as np
        SL, BS, HS = (1024, 4, 512)
        FF = 2048
        E, RANK, TOPK = (8, 64, 2)
        key = jax.random.key(seed)
        ks = jax.random.split(key, 7)
        s = 0.02
        return {'x': jax.random.normal(ks[0], (SL, BS, HS), jnp.float32), 'expert_weights': jax.random.uniform(ks[1], (SL * BS, TOPK), jnp.float32), 'expert_indices': jax.random.randint(ks[2], (SL * BS, TOPK), 0, E).astype(jnp.int32), 'w1_A': jax.random.normal(ks[3], (E * RANK, HS), jnp.float32) * s, 'w1_B': jax.random.normal(ks[4], (E * RANK, FF), jnp.float32) * s, 'w2_A': jax.random.normal(ks[5], (E * RANK, FF), jnp.float32) * s, 'w2_B': jax.random.normal(ks[6], (E * RANK, HS), jnp.float32) * s}
    _L0_ffn_in = _L0_ffn_setup()
    _d = {'L0_attn_x': _L0_attn_in['x'], 'L0_attn_delta': _L0_attn_in['delta'], 'L0_attn_alpha': _L0_attn_in['alpha'], 'L0_attn_beta': _L0_attn_in['beta'], 'L0_attn_gamma': _L0_attn_in['gamma'], 'L0_attn_omega': _L0_attn_in['omega'], 'L0_ffn_expert_weights': _L0_ffn_in['expert_weights'], 'L0_ffn_expert_indices': _L0_ffn_in['expert_indices'], 'L0_ffn_w1_A': _L0_ffn_in['w1_A'], 'L0_ffn_w1_B': _L0_ffn_in['w1_B'], 'L0_ffn_w2_A': _L0_ffn_in['w2_A'], 'L0_ffn_w2_B': _L0_ffn_in['w2_B']}
    _x0 = _d['L0_attn_x']
    _d['L0_attn_x'] = jax.random.normal(jax.random.fold_in(jax.random.key(seed), 1), (8, 4096, 512), dtype=_x0.dtype)
    del _x0
    return _d

def reference(L0_attn_x, L0_attn_delta, L0_attn_alpha, L0_attn_beta, L0_attn_gamma, L0_attn_omega, L0_ffn_expert_weights, L0_ffn_expert_indices, L0_ffn_w1_A, L0_ffn_w1_B, L0_ffn_w2_A, L0_ffn_w2_B):

    def _L0_attn_ref(x, delta, alpha, beta, gamma, omega):
        import jax, jax.numpy as jnp
        import numpy as np
        import math
        B, L, D, N = (8, 2048, 512, 16)
        b, l, d = x.shape
        n_state = gamma.shape[-1]
        scale = math.sqrt(1.0 / n_state)
        residual = x * omega
        xt = jnp.swapaxes(x, -1, -2)
        p = jax.nn.sigmoid(delta)
        a = jax.nn.sigmoid(alpha)
        q = 1.0 - p * a
        t = jnp.arange(l, dtype=x.dtype)
        vander = t[None, None, :] * jnp.log(q)
        kernel = p * beta * jnp.exp(vander)
        k = jnp.einsum('dnl,dn->dl', kernel, gamma * scale)
        n_fft = 2 * l
        k_f = jnp.fft.rfft(k, n=n_fft)
        x_f = jnp.fft.rfft(xt, n=n_fft)
        out = jnp.fft.irfft(x_f * k_f, n=n_fft)[..., :l]
        return jnp.swapaxes(out, -1, -2) + residual

    def _L0_ffn_ref(x, expert_weights, expert_indices, w1_A, w1_B, w2_A, w2_B):
        import jax, jax.numpy as jnp
        import numpy as np
        SL, BS, HS = (1024, 4, 512)
        FF = 2048
        E, RANK, TOPK = (8, 64, 2)
        sl, bs, hs = x.shape
        T = sl * bs
        top_k = expert_indices.shape[-1]
        flat_e = expert_indices.reshape(-1)
        flat_w = expert_weights.reshape(-1)
        order = jnp.argsort(flat_e, stable=True)
        bin_ids = flat_e[order]
        tok = order // top_k
        xr = x.reshape(T, hs)[tok]
        w1A = w1_A.reshape(E, RANK, hs)
        w1B = w1_B.reshape(E, RANK, FF)
        w2A = w2_A.reshape(E, RANK, FF)
        w2B = w2_B.reshape(E, RANK, hs)
        out = jnp.zeros_like(xr)
        for e in range(E):
            mask = (bin_ids == e).astype(xr.dtype)[:, None]
            h = jax.nn.gelu(xr @ w1A[e].T @ w1B[e], approximate=False)
            ye = h @ w2A[e].T @ w2B[e]
            out = out + mask * ye
        y = jnp.zeros((T, hs), xr.dtype).at[tok].add(flat_w[order][:, None] * out)
        return y.reshape(sl, bs, hs)
    x = L0_attn_x
    x = x + _L0_attn_ref(_layernorm(x, axis=-1), L0_attn_delta, L0_attn_alpha, L0_attn_beta, L0_attn_gamma, L0_attn_omega)
    x = x + _L0_ffn_ref(_layernorm(x, axis=-1), L0_ffn_expert_weights, L0_ffn_expert_indices, L0_ffn_w1_A, L0_ffn_w1_B, L0_ffn_w2_A, L0_ffn_w2_B)
    return x

_drawn_inputs = setup_inputs


def setup_inputs(seed=0):
    import zlib

    import numpy as np

    out = dict(_drawn_inputs(seed))
    spreads = {}
    factors = {'L0_ffn_expert_weights': 8.0,
     'L0_ffn_w1_A': 8.0,
     'L0_ffn_w1_B': 8.0,
     'L0_ffn_w2_A': 8.0,
     'L0_ffn_w2_B': 8.0}
    for name, (base, spread) in spreads.items():
        noise = np.random.default_rng([zlib.crc32(name.encode()), seed]).standard_normal(out[name].shape)
        drawn = base * np.exp(spread * noise) if base else spread * noise
        out[name] = jnp.asarray(drawn.astype(out[name].dtype))
    for name, factor in factors.items():
        out[name] = (out[name] * factor).astype(out[name].dtype)
    return out
```

```python
from contextlib import ExitStack

import concourse.bass as bass
from concourse import mybir

F32 = mybir.dt.float32
I32 = mybir.dt.int32
ALU = mybir.AluOpType
ACT = mybir.ActivationFunctionType
AX_X = mybir.AxisListType.X

P = 128
FAR = 1e36
TINY = 1e-30
EPS = 1e-5


def wait(eng, sem, value):
    if isinstance(value, int) and value <= 0:
        return
    eng.wait_ge(sem, value)


def now(eng, *values):
    for v in values:
        if not isinstance(v, int):
            eng.compute_val(v)


def hold(eng, sem, value, met):
    now(eng, value)
    eng.wait_ge(met, 1)
    wait(eng, sem, value)


def build(nc, x, delta, alpha, beta, gamma, omega, ew, ei, w1a, w1b, w2a, w2b, out, ei_experts=8):
    B, L, D = x.shape
    N = gamma.shape[1]
    CH = L // P
    HB = P // CH
    NH = B // HB
    DG = D // P
    R = B * CH
    UC = P // N
    NU = D // UC
    UT = P // UC
    KD = 2 * UC
    NK = D // KD
    BT = UT // 2
    NT = NH * DG
    NB = NT * BT
    NI = P + N
    BANKS = [(0, 3), (3, 6), (6, 8)]
    LR = 8
    LBUF = 4
    NL = R // LR
    assert UC == 8 and NH == 2 and HB * NH == B and NL % LBUF == 0

    E = ei_experts
    RANK = w1a.shape[0] // E
    T = ei.shape[0]
    TK = ei.shape[1]
    FF = w1b.shape[1]
    ER = E * RANK
    KC = D // P
    FC = FF // P
    TT = T // P
    RT = (T * TK + E * (P - 1)) // P
    RT += RT % 2
    NOWHERE = 1 << 20
    assert T <= L and ER == D and RANK == 64 and TK == 2 and TT % 2 == 0 and FC % 4 == 0

    x_rows = x.rearrange("b (c s) d -> s (b c) d", s=P)
    o_rows = out.rearrange("b (c t) d -> (b c) t d", t=P)

    ctx = ExitStack()
    with ctx:
        def sb(name, shape, dt=F32):
            return ctx.enter_context(nc.sbuf_tensor(name, shape, dt))

        def sem(name):
            return ctx.enter_context(nc.semaphore(name))

        taps_d = nc.dram_tensor("taps_d", [NK, 2 * P, KD], F32).ap()
        decay_d = nc.dram_tensor("decay_d", [NK, P, N, KD], F32).ap()

        a_d = nc.dram_tensor("a_d", [T, ER], F32).ap()
        r_d = nc.dram_tensor("r_d", [T, ER], F32).ap()
        slot_d = nc.dram_tensor("slot_d", [RT, P], I32).ap()

        xb = sb("xb", [P, 2, P, P])
        wb = sb("wb", [P, 2, NI, KD])
        raw = sb("raw", [P, 2, UC, P])
        cen = sb("cen", [P, 2, UC, P])
        xn = sb("xn", [P, 2, UC, P])
        far = sb("far", [P, (UC + 1) * P])
        carry = sb("carry", [P, 2, (UC + 1) * P])
        chunk_s = sb("chunk_s", [P, 2, P])
        shift_s = sb("shift_s", [P, 2, HB, CH])
        state = sb("state", [P, 2, P])
        mean = sb("mean", [P, R])
        var = sb("var", [P, R])
        rstd = sb("rstd", [P, R])
        rate = sb("rate", [P, NU])
        coef = sb("coef", [P, NU])
        ident = sb("ident", [P, P])
        own = sb("own", [P, UC])
        back = sb("back", [P, P])
        decay = sb("decay", [P, 2, P])
        last = sb("last", [1, P])
        om = sb("om", [1, D])
        eps = sb("eps", [P, 1])

        raw_row = raw[:].rearrange("p k d r -> p (k d r)")
        cen_row = cen[:].rearrange("p k d r -> p (k d r)")
        xn_row = xn[:].rearrange("p k d r -> p (k d r)")
        stats = raw_row[:, 0:R * 6].rearrange("p (r f) -> p r f", f=6)
        par = cen_row[0:NU, 0:8 * P].rearrange("p (a b) -> p a b", a=8)
        taps = cen_row[:, 8 * P:8 * P + D].rearrange("p (k d) -> p k d", k=NK)
        zero = cen_row[:, 12 * P:12 * P + D].rearrange("p (k d) -> p k d", k=NK)
        coef8 = xn_row[:, 0:D].rearrange("p (u d) -> p u d", u=NU)
        loadbuf = xb[:, 0].rearrange("p a b -> p (a b)").rearrange("p (k r d) -> p k r d", k=LBUF, r=LR)
        decays = xb[:, 1].rearrange("p a b -> p (a b)")[:, 0:D * N].rearrange("p (k n d) -> p k n d", k=NK, n=N)

        xb_all = xb[:].rearrange("p h a b -> p (h a b)")
        wb_row = wb[:].rearrange("p h m d -> p (h m d)")
        load1a = xb_all[:, 0:KC * D].rearrange("p (m d) -> p m d", m=KC)
        load2a = xb_all[:, KC * D:KC * D + KC * FF].rearrange("p (m f) -> p m f", m=KC)
        o = P * P
        w2at = xb_all[:, o:o + FC * ER].rearrange("p (f r) -> p f r", f=FC)
        o += FC * ER
        w1at = xb_all[:, o:o + KC * ER].rearrange("p (k r) -> p k r", k=KC)
        o += KC * ER
        w2bs = xb_all[:, o:o + KC * D].rearrange("p (k d) -> p k d", k=KC)
        o += KC * D
        w1bs = xb_all[0:RANK, o:o + 2 * FF].rearrange("p (k f) -> p k f", k=2)
        assert o + 2 * FF <= 2 * P * P
        act_h = [raw_row.rearrange("p (f r) -> p f r", f=FC), cen_row.rearrange("p (f r) -> p f r", f=FC)]
        tok_x = xn_row[:, 0:2 * D].rearrange("p (k d) -> p k d", k=2)
        tok_n = xn_row[:, 2 * D:4 * D].rearrange("p (k d) -> p k d", k=2)
        tok_t = wb_row[:, 0:2 * D].rearrange("p (k d) -> p k d", k=2)
        tok_a = wb_row[:, 2 * D:4 * D].rearrange("p (k d) -> p k d", k=2)
        zeros_f = carry[:].rearrange("p k c -> p (k c)")[:, 0:4 * D]
        route_a = chunk_s[:, :, 0:RANK]
        route_y = chunk_s[:, :, RANK:2 * RANK]
        route_t = state

        carry_row = carry[:].rearrange("p k c -> p (k c)")
        hot = carry_row[:, 0:3 * E * TT].rearrange("p (k e j) -> p k e j", k=3, e=E)
        o = 3 * E * TT
        rank_in = carry_row[:, o:o + E * TT].rearrange("p (e j) -> p e j", e=E)
        o += E * TT
        tmp_e = carry_row[:, o:o + E * TT].rearrange("p (e j) -> p e j", e=E)
        o += E * TT
        e_of = carry_row[:, o:o + E * TT].rearrange("p (e j) -> p e j", e=E)
        o += E * TT
        tri = carry_row[:, o:o + P]
        o += P
        ones = carry_row[:, o:o + P]
        t_of = xn_row[0:1, D:D + RT * E].rearrange("p (t e) -> p t e", e=E)
        t_le = xn_row[0:1, D + RT * E:D + 2 * RT * E].rearrange("p (t e) -> p t e", e=E)
        slots_f = xb_all[0:RT, 3 * P * P // 4:3 * P * P // 4 + P]

        idx = sb("idx", [P, TT, TK], I32)
        wgt = sb("wgt", [P, TT, TK])
        idf = sb("idf", [P, TT, TK])
        route_w = sb("route_w", [P, E, TT])
        small = sb("small", [P, 8, E])
        smalli = sb("smalli", [P, E], I32)
        posf = sb("posf", [P, TK, TT])
        rowf = sb("rowf", [P, TK, TT])
        posi = sb("posi", [P, TK, TT], I32)
        rowi = sb("rowi", [P, TK, TT], I32)
        flag = sb("flag", [P, TT])
        tok8 = sb("tok8", [P, TT])
        t_ef = sb("t_ef", [1, RT])
        t_e = sb("t_e", [1, RT], I32)
        slots_i = sb("slots_i", [RT, P], I32)
        slots = sb("slots", [P, RT], I32)
        stage_p = sb("stage_p", [P, 2, TK], I32)
        stage_r = sb("stage_r", [P, 2, TK], I32)
        pick_g = sb("pick_g", [P, 2], I32)
        pick_s = sb("pick_s", [P, 2], I32)
        tstat = sb("tstat", [P, 2, 12])

        ps = ctx.enter_context(nc.psum_tensor("ps", [P, 8, 512], F32))

        s_par = sem("s_par")
        s_om = sem("s_om")
        s_const = sem("s_const")
        s_prep = sem("s_prep")
        s_tap = sem("s_tap")
        s_exp = sem("s_exp")
        s_cp = sem("s_cp")
        s_tab = sem("s_tab")
        s_load = [sem(f"s_load{k}") for k in range(LBUF)]
        s_free = sem("s_free")
        s_dv = sem("s_dv")
        s_std = sem("s_std")
        s_x = sem("s_x")
        s_w = sem("s_w")
        s_cen = sem("s_cen")
        s_raw = sem("s_raw")
        s_xn = sem("s_xn")
        s_loc = sem("s_loc")
        s_cs = sem("s_cs")
        s_tr = sem("s_tr")
        s_sh = sem("s_sh")
        s_ca = sem("s_ca")
        s_st = sem("s_st")
        s_pe = sem("s_pe")
        s_ev = sem("s_ev")
        s_out = sem("s_out")

        s_idx = sem("s_idx")
        s_rt = sem("s_rt")
        s_rp = sem("s_rp")
        s_slot0 = sem("s_slot0")
        s_stg = sem("s_stg")
        s_scat = [sem(f"s_scat{k}") for k in range(2)]
        s_sf = sem("s_sf")
        s_slots = sem("s_slots")
        s_wl = sem("s_wl")
        s_wt = sem("s_wt")
        s_wc = sem("s_wc")
        s_zero = sem("s_zero")
        s_zf = sem("s_zf")
        s_tx = [sem(f"s_tx{k}") for k in range(2)]
        s_tv = sem("s_tv")
        s_ts = sem("s_ts")
        s_tn = sem("s_tn")
        s_tt = sem("s_tt")
        s_tc = sem("s_tc")
        s_ta = sem("s_ta")
        s_tb = sem("s_tb")
        s_td = [sem(f"s_td{k}") for k in range(2)]
        s_ch = sem("s_ch")
        s_pg = sem("s_pg")
        s_g = [sem(f"s_g{k}") for k in range(2)]
        s_gt = sem("s_gt")
        s_gc = sem("s_gc")
        s_wu = [sem(f"s_wu{k}") for k in range(2)]
        s_up = sem("s_up")
        s_ge = sem("s_ge")
        s_dn = sem("s_dn")
        s_y = sem("s_y")
        s_pk = sem("s_pk")
        s_s = [sem(f"s_s{k}") for k in range(2)]
        s_rx = [sem(f"s_rx{k}") for k in range(2)]
        s_rw = sem("s_rw")
        s_r1 = sem("s_r1")
        s_r2 = sem("s_r2")
        s_r3 = sem("s_r3")
        s_r4 = sem("s_r4")
        s_r5 = [sem(f"s_r5{k}") for k in range(2)]

        NCONST = 28
        NROUTE = 47
        DV_STATS = 9

        block = ctx.enter_context(nc.Block())

        def tile_half(i):
            return (i // BT) % 2

        def unit_of(i, k):
            return (i // (2 * BT)) * UT + (i % BT) * 2 + k

        def unit_cols(eng, i, k):
            v = tile_half(i) * (P * P) + (i % BT) * KD + k * UC
            return v if isinstance(v, int) else eng.snap(v)

        xb_row = xb[:].rearrange("p h a b -> p (h a) b")

        def unit_view(eng, i, k):
            row = tile_half(i) * P
            col = (i % BT) * KD + k * UC
            if not isinstance(i, int):
                row, col = eng.snap(row), eng.snap(col)
            return xb_row[:, bass.ds(row, P), bass.ds(col, UC)]

        def in_pairs(eng, n, step, later=None):
            def pair(q):
                for k in range(2):
                    if later is not None and not (isinstance(q, int) and q == 0):
                        later(q * 2 - 2 + k, k)
                    step(q * 2 + k, k)

            pair(0)
            pair(1)
            with eng.Fori(2, n // 2) as q:
                pair(q)
            if later is not None:
                later(n - 2, 0)
                later(n - 1, 1)

        def over_blocks(eng, step):
            step(0, True, False)
            with eng.Fori(1, NB - 1) as i:
                step(i, False, False)
            step(NB - 1, False, True)

        @block.gpsimd
        def _(pool):
            n = 0

            def const(ins):
                nonlocal n
                n += 1
                ins.then_inc(s_const, 1)
                pool.wait_ge(s_const, n)

            const(pool.memset(ident[:], 1.0))
            const(pool.affine_select(out=ident[:], in_=ident[:], compare_op=ALU.is_equal, fill=0.0,
                                     base=0, pattern=[[-1, P]], channel_multiplier=1))
            const(pool.memset(own[:], 1.0))
            const(pool.affine_select(out=own[:], in_=own[:], compare_op=ALU.is_ge, fill=0.0,
                                     base=0, pattern=[[-N, UC]], channel_multiplier=1))
            const(pool.affine_select(out=own[:], in_=own[:], compare_op=ALU.is_ge, fill=0.0,
                                     base=N - 1, pattern=[[N, UC]], channel_multiplier=-1))
            const(pool.iota(back[:], pattern=[[-1, P]], base=P - 1, channel_multiplier=0,
                            allow_small_or_imprecise_dtypes=True))
            const(pool.memset(last[:], 0.0))
            const(pool.memset(last[:, P - 1:P], 1.0))
            const(pool.memset(zero, 0.0))
            const(pool.memset(eps[:], EPS))
            cv = far[:, 0:UC * P].rearrange("p (j t) -> p j t", j=UC)
            const(pool.iota(cv, pattern=[[0, UC], [1, P]], base=1, channel_multiplier=0,
                            allow_small_or_imprecise_dtypes=True))
            const(pool.affine_select(out=cv, in_=cv, compare_op=ALU.is_ge, fill=FAR,
                                     base=0, pattern=[[-N, UC], [0, P]], channel_multiplier=1))
            const(pool.affine_select(out=cv, in_=cv, compare_op=ALU.is_ge, fill=FAR,
                                     base=N - 1, pattern=[[N, UC], [0, P]], channel_multiplier=-1))
            const(pool.memset(far[:, UC * P:], float(P)))
            const(pool.memset(far[:, UC * P:].rearrange("p (b c) -> p b c", b=HB)[:, :, 0:1], FAR))
            const(pool.memset(shift_s[:], 0.0))

            const(pool.iota(e_of, pattern=[[1, E], [0, TT]], base=0, channel_multiplier=0,
                            allow_small_or_imprecise_dtypes=True))
            const(pool.iota(tok8[:], pattern=[[E, TT]], base=0, channel_multiplier=E * TT,
                            allow_small_or_imprecise_dtypes=True))
            const(pool.memset(ones, 1.0))
            const(pool.memset(tri, 1.0))
            const(pool.affine_select(out=tri, in_=tri, compare_op=ALU.is_gt, fill=0.0,
                                     base=0, pattern=[[1, P]], channel_multiplier=-1))
            const(pool.iota(t_of, pattern=[[1, RT], [0, E]], base=0, channel_multiplier=0,
                            allow_small_or_imprecise_dtypes=True))
            const(pool.memset(slots_i[:], NOWHERE))
            const(pool.memset(pick_g[:], NOWHERE))
            const(pool.memset(pick_s[:], NOWHERE))
            const(pool.memset(stage_p[:], NOWHERE))
            const(pool.memset(stage_r[:], NOWHERE))
            const(pool.memset(t_e[:], 0))

            pool.wait_ge(s_rt, NROUTE)
            pool.wait_ge(s_slot0, 16)

            def send(j, k):
                jj = j if isinstance(j, int) else pool.snap(j)
                wait(pool, s_scat[k], 16 * TK * (j // 2))
                pool.tensor_copy(stage_p[:, k, :], posi[:, :, bass.ds(jj, 1)].rearrange("p k j -> p (k j)"))\
                    .then_inc(s_stg, 1)
                pool.tensor_copy(stage_r[:, k, :], rowi[:, :, bass.ds(jj, 1)].rearrange("p k j -> p (k j)"))\
                    .then_inc(s_stg, 1)
                hold(pool, s_stg, 2 * (j + 1), s_const)
                for c in range(TK):
                    pool.indirect_dma_start(
                        out=slot_d.rearrange("a b -> (a b)")[:, None],
                        out_offset=bass.IndirectOffsetOnAxis(ap=stage_p[:, k, c:c + 1], axis=0),
                        in_=stage_r[:, k, c:c + 1], in_offset=None,
                        bounds_check=RT * P - 1, oob_is_err=False).then_inc(s_scat[k], 16)

            in_pairs(pool, TT, send)

            pool.wait_ge(s_dv, DV_STATS)

            def centre(i, first, final):
                for k in range(2):
                    u = 2 * i + k
                    wait(pool, s_x, (i // BT + 1) * 16)
                    wait(pool, s_xn, u - 1)
                    h = tile_half(i) * P
                    if not isinstance(i, int):
                        h = pool.snap(h)
                    pool.tensor_tensor(cen[:, k].rearrange("p d r -> p r d"), unit_view(pool, i, k),
                                       mean[:, bass.ds(h, P)][:, :, None].to_broadcast([P, P, UC]),
                                       ALU.subtract).then_inc(s_cen, 1)

            over_blocks(pool, centre)

            for k in range(2):
                pool.wait_ge(s_td[k], 16 * (TT // 2))
            pool.wait_ge(s_sf, 3)
            pool.wait_ge(s_zero, 16 * (TT // 4))
            pool.wait_ge(s_zf, 2)

            def gather(t, k):
                tt = t if isinstance(t, int) else pool.snap(t)
                wait(pool, s_g[k], 16 * (t // 2))
                wait(pool, s_gt, t - 1)
                pool.tensor_copy(pick_g[:, k:k + 1], slots[:, bass.ds(tt, 1)]).then_inc(s_pg, 1)
                hold(pool, s_pg, t + 1, s_const)
                pool.indirect_dma_start(
                    out=route_a[:, k, :], out_offset=None, in_=a_d.rearrange("t (e r) -> (t e) r", e=E),
                    in_offset=bass.IndirectOffsetOnAxis(ap=pick_g[:, k:k + 1], axis=0),
                    bounds_check=T * E - 1, oob_is_err=False).then_inc(s_g[k], 16)

            def scatter(t, k):
                tt = t if isinstance(t, int) else pool.snap(t)
                wait(pool, s_s[k], 16 * (t // 2))
                pool.tensor_copy(pick_s[:, k:k + 1], slots[:, bass.ds(tt, 1)]).then_inc(s_pk, 1)
                hold(pool, s_pk, t + 1, s_const)
                wait(pool, s_y, t + 1)
                pool.indirect_dma_start(
                    out=r_d.rearrange("t (e r) -> (t e) r", e=E),
                    out_offset=bass.IndirectOffsetOnAxis(ap=pick_s[:, k:k + 1], axis=0),
                    in_=route_y[:, k, :], in_offset=None,
                    bounds_check=T * E - 1, oob_is_err=False).then_inc(s_s[k], 16)

            gather(0, 0)
            gather(1, 1)
            gather(2, 0)
            scatter(0, 0)
            gather(3, 1)
            scatter(1, 1)
            with pool.Fori(2, RT // 2) as q:
                for k in range(2):
                    gather(q * 2 + k, k)
                    scatter(q * 2 - 2 + k, k)
            scatter(RT - 2, 0)
            scatter(RT - 1, 1)

        @block.sync
        def _(sp):
            for j, a in enumerate((delta, alpha, beta)):
                sp.dma_start(par[:, j, :], a.rearrange("(u d) n o -> u (d n o)", d=UC)).then_inc(s_par, 16)
            sp.dma_start(par[:, 3, :], gamma.rearrange("(u d) n -> u (d n)", d=UC)).then_inc(s_par, 16)
            sp.dma_start(om[:], omega.rearrange("(a d) -> a d", a=1)).then_inc(s_om, 16)
            sp.dma_start(idx[:], ei.rearrange("(p j) k -> p j k", p=P)).then_inc(s_idx, 16)
            sp.dma_start(wgt[:], ew.rearrange("(p j) k -> p j k", p=P)).then_inc(s_idx, 16)
            for k in range(LBUF):
                sp.dma_start(loadbuf[:, k], x_rows[:, k * LR:(k + 1) * LR, :]).then_inc(s_load[k], 16)
            with sp.Fori(1, NL // LBUF) as q:
                for k in range(LBUF):
                    at = sp.snap(q * (LBUF * LR) + k * LR)
                    sp.wait_ge(s_free, sp.snap((q - 1) * LBUF + k + 1))
                    sp.dma_start(loadbuf[:, k], x_rows[:, bass.ds(at, LR), :])\
                        .then_inc(s_load[k], 16)
            sp.wait_ge(s_const, NCONST)
            sp.dma_start(slot_d, slots_i[:]).then_inc(s_slot0, 16)
            sp.wait_ge(s_cp, NK)
            sp.dma_start(taps_d[:, 0:P, :].rearrange("k i d -> i k d"), taps).then_inc(s_tab, 16)
            sp.dma_start(taps_d[:, P:2 * P, :].rearrange("k i d -> i k d"), zero).then_inc(s_tab, 16)
            sp.dma_start(decay_d.rearrange("k s n d -> s k (n d)"),
                         decays.rearrange("p k n d -> p k (n d)")).then_inc(s_tab, 16)
            sp.wait_ge(s_tab, 48)

            def load_tile(t, after, value):
                dg, h = t // 2, t % 2
                r0, d0 = h * P, dg * P
                if not isinstance(t, int):
                    r0, d0 = sp.snap(r0), sp.snap(d0)
                dst = xb_row[:, bass.ds(r0, P), :]
                src = x_rows[:, bass.ds(r0, P), bass.ds(d0, P)]
                wait(sp, after, value)
                sp.dma_start(dst, src).then_inc(s_x, 16)

            def store_tile(t, after, value):
                dg, h = t // 2, t % 2
                r0, d0 = h * P, dg * P
                if not isinstance(t, int):
                    r0, d0 = sp.snap(r0), sp.snap(d0)
                src = xb_row[:, bass.ds(r0, P), :]
                dst = o_rows[bass.ds(r0, P), :, bass.ds(d0, P)]
                wait(sp, after, value)
                sp.dma_start(dst, src).then_inc(s_out, 16)

            def load_weights(i):
                kb = (i // (2 * BT)) * BT + i % BT
                h = i % 2
                if not isinstance(i, int):
                    kb, h = sp.snap(kb), sp.snap(h)
                dst = wb[:, bass.ds(h, 1)].rearrange("p h m d -> p (h m) d")
                row = taps_d[bass.ds(kb, 1)].rearrange("k i d -> k (i d)")
                src = bass.AP(row.tensor, row.offset, [[KD, P], [1, P * KD]])
                dec = decay_d[bass.ds(kb, 1)].rearrange("k s n d -> (k s) n d")
                loads, read = 32 * i, 2 * (i - 1)
                now(sp, loads, read)
                wait(sp, s_w, loads)
                wait(sp, s_loc, read)
                sp.dma_start(dst[:, N:, :], src).then_inc(s_w, 16)
                sp.dma_start(dst[:, 0:N, :], dec).then_inc(s_w, 16)

            load_tile(0, s_dv, DV_STATS)

            def tile(t, first, final):
                for b in range(BT):
                    if b == 2 and not first:
                        store_tile(t - 1, s_ev, 3 * UT * t)
                    if b == 1 and first:
                        load_tile(1, s_x, 16)
                    if b == 5 and not first and not final:
                        load_tile(t + 1, s_out, 16 * t)
                    load_weights(t * BT + b)

            tile(0, True, False)
            with sp.Fori(1, NT - 1) as t:
                tile(t, False, False)
            tile(NT - 1, False, True)
            store_tile(NT - 1, s_ev, 3 * UT * NT)
            sp.wait_ge(s_out, 16 * NT)

            sp.wait_ge(s_pe, 3 * UT * NT)
            sp.dma_start(load1a, w1a.rearrange("(m p) d -> p m d", p=P)).then_inc(s_wl, 16)
            sp.dma_start(load2a, w2a.rearrange("(m p) f -> p m f", p=P)).then_inc(s_wl, 16)
            sp.dma_start(w2bs, w2b.rearrange("(k p) d -> p k d", p=P)).then_inc(s_wl, 16)
            for k in range(2):
                sp.wait_ge(s_scat[k], 16 * TK * (TT // 2))
            sp.dma_start(slots_i[:], slot_d).then_inc(s_slots, 16)
            sp.wait_ge(s_zf, 1)
            for q in range(TT // 4):
                sp.dma_start(r_d.rearrange("(q p a) r -> q p (a r)", p=P, a=4)[q], zeros_f).then_inc(s_zero, 16)

            x_tok = out.rearrange("b l d -> (b l) d")[0:T].rearrange("(p j) d -> j p d", j=TT)
            a_tok = a_d.rearrange("(p j) r -> j p r", j=TT)
            r_tok = r_d.rearrange("(p j) r -> j p r", j=TT)

            def one(ap, j):
                if not isinstance(j, int):
                    j = sp.snap(j)
                return ap[bass.ds(j, 1)].rearrange("a p d -> (a p) d")

            def tok_load(j, k):
                wait(sp, s_tn, j - 1)
                sp.dma_start(tok_x[:, k, :], one(x_tok, j)).then_inc(s_tx[k], 16)

            def tok_store(j, k):
                v = one(a_tok, j)
                wait(sp, s_tb, j + 1)
                sp.dma_start(v, tok_a[:, k, :]).then_inc(s_td[k], 16)

            in_pairs(sp, TT, tok_load, tok_store)

            def up_load(t, k):
                tt = t if isinstance(t, int) else sp.snap(t)
                e = sp.value_load(t_e[0:1, bass.ds(tt, 1)], min_val=0, max_val=E - 1)
                row = sp.snap(e * RANK)
                wait(sp, s_up, 4 * (t - 1))
                sp.dma_start(w1bs[:, k, :], w1b[bass.ds(row, RANK), :]).then_inc(s_wu[k], 16)

            in_pairs(sp, RT, up_load)

            for k in range(2):
                sp.wait_ge(s_s[k], 16 * (RT // 2))

            def res_load(j, k):
                v, w = one(r_tok, j), one(x_tok, j)
                wait(sp, s_r5[k], 16 * (j // 2))
                wait(sp, s_rw, j - 1)
                sp.dma_start(tok_a[:, k, :], v).then_inc(s_rx[k], 16)
                sp.dma_start(tok_x[:, k, :], w).then_inc(s_rx[k], 16)

            def res_store(j, k):
                v = one(x_tok, j)
                wait(sp, s_r4, j + 1)
                sp.dma_start(v, tok_x[:, k, :]).then_inc(s_r5[k], 16)

            in_pairs(sp, TT, res_load, res_store)
            for k in range(2):
                sp.wait_ge(s_r5[k], 16 * (TT // 2))

        @block.scalar
        def _(act):
            act.wait_ge(s_par, 64)
            act.activation(par[:, 4, :], par[:, 0, :], ACT.Sigmoid).then_inc(s_prep, 1)
            act.activation(par[:, 5, :], par[:, 1, :], ACT.Sigmoid).then_inc(s_prep, 1)
            act.wait_ge(s_prep, 4)
            act.activation(par[:, 7, :], par[:, 6, :], ACT.Ln).then_inc(s_prep, 1)
            act.wait_ge(s_prep, 11)

            def table(i, first, final):
                for k in range(2):
                    u = 2 * i + k
                    if not first:
                        wait(act, s_tap, i)
                    col = u if isinstance(u, int) else act.snap(u)
                    act.activation(decay[:, k, :], back[:], ACT.Exp, scale=rate[:, bass.ds(col, 1)])\
                       .then_inc(s_exp, 1)
                ii = i if isinstance(i, int) else act.snap(i)
                act.wait_ge(s_tap, (i + 1) if isinstance(i, int) else act.snap(i + 1))
                act.activation(taps[:, bass.ds(ii, 1), :].rearrange("p k d -> p (k d)"), ps[:, 0, 0:KD],
                               ACT.Copy)
                for k in range(2):
                    dst = decays[:, bass.ds(ii, 1), :, k * UC:(k + 1) * UC].rearrange("p k n d -> p (k n) d")
                    ins = act.activation(dst.rearrange("p n d -> p d n"),
                                         ps[:, 1, k * P:(k + 1) * P].rearrange("p (d n) -> p d n", d=UC)[:, :, ::-1],
                                         ACT.Copy)
                ins.then_inc(s_cp, 1)

            act.wait_ge(s_const, NCONST)
            table(0, True, False)
            with act.Fori(1, NK) as i:
                table(i, False, False)
            act.wait_ge(s_dv, DV_STATS - 1)
            act.activation(rstd[:], var[:], ACT.Sqrt, bias=eps[:, 0:1]).then_inc(s_std, 1)

            def evacuate(i, k):
                u = 2 * i + k
                view = unit_view(act, i, k)
                for b, (a, z) in enumerate(BANKS):
                    wait(act, s_pe, 3 * u + b + 1)
                    act.activation(view[:, :, a:z].rearrange("p t d -> p d t"),
                                   ps[:, 3 * k + b, 0:NI * (z - a)].rearrange("p (d t) -> p d t", t=NI)[:, :, 0:P],
                                   ACT.Copy).then_inc(s_ev, 1)

            def steps(i, first, final):
                for k in range(2):
                    u = 2 * i + k
                    col = unit_of(i, k)
                    if not isinstance(i, int):
                        col = act.snap(col)
                    wait(act, s_pe, 3 * (u - 1))
                    act.activation(carry[:, k, :], far[:], ACT.Exp, scale=rate[:, bass.ds(col, 1)])\
                       .then_inc(s_ca, 1)
                    if not (first and k == 0):
                        evacuate(i if k == 1 else i - 1, 1 - k)
                    wait(act, s_tr, u + 2)
                    wait(act, s_st, u - 1)
                    act.activation(shift_s[:, k, :, 1:CH],
                                   ps[:, 6 + k, 0:P].rearrange("p (b c) -> p b c", b=HB)[:, :, 0:CH - 1],
                                   ACT.Copy, scale=coef[:, bass.ds(col, 1)]).then_inc(s_sh, 1)

            over_blocks(act, steps)
            evacuate(NB - 1, 1)

            for c in range(KC + FC):
                dst = w1at[:, c, :] if c < KC else w2at[:, c - KC, :]
                act.wait_ge(s_wt, c + 1)
                act.activation(dst, ps[:, c % 2, :], ACT.Copy).then_inc(s_wc, 1)

            def tokens(j, k):
                wait(act, s_tv, j + 1)
                act.activation(tstat[:, k, 8:9], tstat[:, k, 7:8], ACT.Sqrt, bias=eps[:, 0:1]).then_inc(s_ts, 1)
                wait(act, s_tt, j + 1)
                act.activation(tok_t[:, k, :], ps[:, k, :], ACT.Copy).then_inc(s_tc, 1)

            in_pairs(act, TT, tokens)

            def gelus(t, k):
                for b in range(4):
                    wait(act, s_up, 4 * t + b + 1)
                    if b == 0:
                        wait(act, s_dn, t - 1)
                    n4 = FC // 4
                    act.activation(act_h[k][:, b * n4:(b + 1) * n4, :].rearrange("p f r -> p (f r)"),
                                   ps[:, b, :], ACT.Gelu).then_inc(s_ge, 1)

            in_pairs(act, RT, gelus)

            def results(j, k):
                wait(act, s_r1, j + 1)
                act.activation(tok_t[:, k, :], ps[:, k, :], ACT.Copy).then_inc(s_r2, 1)

            in_pairs(act, TT, results)

        @block.vector
        def _(dve):
            dve.wait_ge(s_prep, 2)
            dve.tensor_tensor(par[:, 6, :], par[:, 4, :], par[:, 5, :], ALU.mult).then_inc(s_prep, 1)
            dve.wait_ge(s_prep, 3)
            dve.tensor_scalar(par[:, 6, :], par[:, 6, :], -1.0, 1.0, ALU.mult, ALU.add).then_inc(s_prep, 1)
            dve.wait_ge(s_prep, 5)
            dve.tensor_scalar(par[:, 7, :], par[:, 7, :], -TINY, None, ALU.min).then_inc(s_prep, 1)
            dve.tensor_tensor(par[:, 4, :], par[:, 4, :], par[:, 2, :], ALU.mult).then_inc(s_prep, 1)
            dve.wait_ge(s_prep, 7)
            dve.tensor_scalar(par[:, 3, :], par[:, 3, :], (1.0 / N) ** 0.5, None, ALU.mult).then_inc(s_prep, 1)
            dve.wait_ge(s_prep, 8)
            dve.tensor_tensor(par[:, 4, :], par[:, 4, :], par[:, 3, :], ALU.mult).then_inc(s_prep, 1)
            dve.wait_ge(s_tr, 1)
            dve.tensor_copy(rate[:], ps[:, 2, 0:NU]).then_inc(s_prep, 1)
            dve.tensor_copy(coef[:], ps[:, 2, NU:2 * NU]).then_inc(s_prep, 1)
            dve.wait_ge(s_prep, 11)
            dve.wait_ge(s_const, NCONST)
            dve.tensor_tensor(coef8, coef[:][:, :, None].to_broadcast([P, NU, UC]),
                              own[:][:, None, :].to_broadcast([P, NU, UC]), ALU.mult).then_inc(s_prep, 1)

            n = 0

            def rt(ins):
                nonlocal n
                n += 1
                ins.then_inc(s_rt, 1)
                dve.wait_ge(s_rt, n)

            def over_e(ap):
                return ap[:, :, None].to_broadcast([P, E, TT])

            def over_t(ap):
                return ap[:, None, :].to_broadcast([P, E, TT])

            dve.wait_ge(s_idx, 32)
            rt(dve.tensor_copy(idf[:], idx[:]))
            for k in range(TK):
                rt(dve.tensor_tensor(hot[:, k], over_t(idf[:, :, k]), e_of, ALU.is_equal))
            rt(dve.tensor_tensor(hot[:, 2], hot[:, 0], hot[:, 1], ALU.max))
            rt(dve.tensor_tensor(route_w[:], hot[:, 0], over_t(wgt[:, :, 0]), ALU.mult))
            rt(dve.tensor_tensor(tmp_e, hot[:, 1], over_t(wgt[:, :, 1]), ALU.mult))
            rt(dve.tensor_tensor(route_w[:], route_w[:], tmp_e, ALU.add))
            for e in range(E):
                rt(dve.tensor_tensor_scan(rank_in[:, e, :], ones[:, 0:TT], hot[:, 2, e, :], 0.0,
                                          ALU.mult, ALU.add))
            rt(dve.tensor_copy(small[:, 0, :], rank_in[:, :, TT - 1]))
            dve.wait_ge(s_rp, 1)
            rt(dve.tensor_copy(small[:, 1, :], ps[:, 3, 0:E]))
            rt(dve.tensor_scalar(smalli[:], ps[:, 3, E:2 * E], float(P - 1), None, ALU.add))
            rt(dve.tensor_scalar(smalli[:], smalli[:], P.bit_length() - 1, None, ALU.arith_shift_right))
            rt(dve.tensor_copy(small[:, 2, :], smalli[:]))
            rt(dve.tensor_tensor_scan(small[:, 3, :], ones[:, 0:E], small[:, 2, :], 0.0, ALU.mult, ALU.add))
            rt(dve.tensor_tensor(small[:, 4, :], small[:, 3, :], small[:, 2, :], ALU.subtract))
            rt(dve.tensor_scalar(small[:, 4, :], small[:, 4, :], float(P), -1.0, ALU.mult, ALU.add))
            rt(dve.tensor_tensor(small[:, 4, :], small[:, 4, :], small[:, 1, :], ALU.add))
            rt(dve.tensor_tensor(rank_in, rank_in, over_e(small[:, 4, :]), ALU.add))
            for k in range(TK):
                rt(dve.tensor_reduce(flag[:], hot[:, k].rearrange("p e j -> p j e"), AX_X, ALU.add))
                rt(dve.tensor_scalar(flag[:], flag[:], -float(NOWHERE), float(NOWHERE), ALU.mult, ALU.add))
                rt(dve.tensor_tensor(tmp_e, hot[:, k], rank_in, ALU.mult))
                rt(dve.tensor_reduce(posf[:, k, :], tmp_e.rearrange("p e j -> p j e"), AX_X, ALU.add))
                rt(dve.tensor_tensor(posf[:, k, :], posf[:, k, :], flag[:], ALU.add))
                rt(dve.tensor_tensor(rowf[:, k, :], idf[:, :, k], tok8[:], ALU.add))
            rt(dve.tensor_tensor(tmp_e, hot[:, 0], hot[:, 1], ALU.mult))
            rt(dve.tensor_reduce(flag[:], tmp_e.rearrange("p e j -> p j e"), AX_X, ALU.add))
            rt(dve.tensor_scalar(flag[:], flag[:], float(NOWHERE), None, ALU.mult))
            rt(dve.tensor_tensor(posf[:, 1, :], posf[:, 1, :], flag[:], ALU.add))
            rt(dve.tensor_copy(posi[:], posf[:]))
            rt(dve.tensor_copy(rowi[:], rowf[:]))
            rt(dve.tensor_tensor(t_le, small[0:1, 3, :][:, None, :].to_broadcast([1, RT, E]), t_of,
                                 ALU.is_le))
            rt(dve.tensor_reduce(t_ef[:], t_le, AX_X, ALU.add))
            rt(dve.tensor_scalar(t_ef[:], t_ef[:], float(E - 1), None, ALU.min))
            rt(dve.tensor_copy(t_e[:], t_ef[:]))
            assert n == NROUTE, n

            def row_stats(q):
                for k in range(LBUF):
                    wait(dve, s_load[k], 16 * (q + 1))
                    for r in range(LR):
                        at = q * (LBUF * LR) + k * LR + r
                        if not isinstance(q, int):
                            at = dve.snap(at)
                        ins = dve.bn_stats(stats[:, bass.ds(at, 1), :].rearrange("p a b -> p (a b)"),
                                           loadbuf[:, k, r, :])
                    ins.then_inc(s_free, 1)

            row_stats(0)
            with dve.Fori(1, NL // LBUF) as q:
                row_stats(q)
            dve.wait_ge(s_free, NL)
            n = 0

            def chain(ins):
                nonlocal n
                n += 1
                ins.then_inc(s_dv, 1)
                dve.wait_ge(s_dv, n)

            st = stats.rearrange("p r f -> p f r")
            chain(dve.tensor_tensor(mean[:], st[:, 1, :], st[:, 4, :], ALU.add))
            chain(dve.tensor_scalar(mean[:], mean[:], 0.5, None, ALU.mult))
            chain(dve.tensor_tensor(rstd[:], st[:, 1, :], st[:, 4, :], ALU.subtract))
            chain(dve.tensor_tensor(rstd[:], rstd[:], rstd[:], ALU.mult))
            chain(dve.tensor_scalar(rstd[:], rstd[:], D / 4.0, None, ALU.mult))
            chain(dve.tensor_tensor(rstd[:], rstd[:], st[:, 2, :], ALU.add))
            chain(dve.tensor_tensor(rstd[:], rstd[:], st[:, 5, :], ALU.add))
            chain(dve.tensor_scalar(var[:], rstd[:], 1.0 / D, None, ALU.mult))
            dve.wait_ge(s_std, 1)
            chain(dve.reciprocal(rstd[:], rstd[:]))
            assert n == DV_STATS

            def stage(i, k):
                u = 2 * i + k
                wait(dve, s_x, (i // BT + 1) * 16)
                wait(dve, s_loc, u - 1)
                dve.tensor_copy(raw[:, k].rearrange("p d r -> p r d"), unit_view(dve, i, k)).then_inc(s_raw, 1)
                wait(dve, s_cen, u + 1)
                h = tile_half(i) * P
                if not isinstance(i, int):
                    h = dve.snap(h)
                dve.tensor_tensor(xn[:, k], cen[:, k],
                                  rstd[:, bass.ds(h, P)][:, None, :].to_broadcast([P, UC, P]),
                                  ALU.mult).then_inc(s_xn, 1)

            def steps(i, first, final):
                for k in range(2):
                    u = 2 * i + k
                    if not (final and k == 1):
                        stage(i if k == 0 else i + 1, 1 - k)
                    wait(dve, s_loc, u + 1)
                    wait(dve, s_tr, u)
                    dst = chunk_s[:, k, :].rearrange("p (d n) -> p d n", n=N)
                    src = ps[:, 3 * k:3 * k + 2, 0:3 * NI].rearrange("p a (d m) -> p a d m", m=NI)[:, :, :, P:]
                    dve.tensor_copy(dst[:, 0:6].rearrange("p (a d) n -> p a d n", a=2), src).then_inc(s_cs, 1)
                    src = ps[:, 3 * k + 2, 0:2 * NI].rearrange("p (d m) -> p d m", m=NI)[:, :, P:]
                    dve.tensor_copy(dst[:, 6:8], src).then_inc(s_cs, 1)
                    wait(dve, s_sh, u + 1)
                    wait(dve, s_ca, u + 1)
                    wait(dve, s_pe, 3 * (u - 1))
                    dve.tensor_tensor_scan(state[:, k, :], carry[:, k, UC * P:],
                                           shift_s[:, k].rearrange("p b c -> p (b c)"), 0.0,
                                           ALU.mult, ALU.add).then_inc(s_st, 1)

            stage(0, 0)
            over_blocks(dve, steps)

            dve.wait_ge(s_pe, 3 * UT * NT)
            dve.memset(zeros_f, 0.0).then_inc(s_zf, 1)
            dve.memset(route_a, 0.0).then_inc(s_zf, 1)
            dve.wait_ge(s_slots, 16)
            dve.tensor_copy(slots_f, slots_i[:]).then_inc(s_sf, 1)
            dve.wait_ge(s_sf, 2)
            dve.tensor_copy(slots[:], ps[:, 4, 0:RT]).then_inc(s_sf, 1)

            def tokens(j, k):
                st, m = tstat[:, k, 0:6], tstat[:, k, 6:8]
                wait(dve, s_tx[k], 16 * (j // 2 + 1))
                dve.bn_stats(st, tok_x[:, k, :]).then_inc(s_ch, 1)
                hold(dve, s_ch, 2 * j + 1, s_const)
                dve.bn_aggr(m, st).then_inc(s_tv, 1)
                wait(dve, s_ts, j + 1)
                dve.reciprocal(tstat[:, k, 9:10], tstat[:, k, 8:9]).then_inc(s_ch, 1)
                wait(dve, s_ch, 2 * j + 2)
                wait(dve, s_tt, j - 1)
                dve.tensor_scalar(tok_n[:, k, :], tok_x[:, k, :], tstat[:, k, 6:7], tstat[:, k, 9:10],
                                  ALU.subtract, ALU.mult).then_inc(s_tn, 1)

            def ranks(j, k):
                wait(dve, s_ta, j + 1)
                wait(dve, s_td[k], 16 * (j // 2))
                dve.tensor_copy(tok_a[:, k, :], ps[:, 2 + k, :]).then_inc(s_tb, 1)

            in_pairs(dve, TT, tokens, ranks)

            def routes_in(t, k):
                wait(dve, s_gt, t + 1)
                wait(dve, s_up, 4 * (t - 1))
                dve.tensor_copy(route_t[0:RANK, k, :], ps[0:RANK, 6 + k, 0:P]).then_inc(s_gc, 1)

            def routes_out(t, k):
                wait(dve, s_dn, t + 1)
                wait(dve, s_s[k], 16 * (t // 2))
                dve.tensor_copy(route_y[:, k, :], ps[:, 4 + k, 0:RANK]).then_inc(s_y, 1)

            routes_in(0, 0)
            routes_in(1, 1)
            routes_in(2, 0)
            routes_out(0, 0)
            routes_in(3, 1)
            routes_out(1, 1)
            with dve.Fori(2, RT // 2) as q:
                for k in range(2):
                    routes_in(q * 2 + k, k)
                    routes_out(q * 2 - 2 + k, k)
            routes_out(RT - 2, 0)
            routes_out(RT - 1, 1)

            def weigh(j, k):
                jj = j if isinstance(j, int) else dve.snap(j)
                wait(dve, s_rx[k], 32 * (j // 2 + 1))
                wait(dve, s_r1, j - 1)
                dve.tensor_tensor(tok_n[:, k, :].rearrange("p (e r) -> p e r", e=E),
                                  tok_a[:, k, :].rearrange("p (e r) -> p e r", e=E),
                                  route_w[:, :, bass.ds(jj, 1)].to_broadcast([P, E, RANK]),
                                  ALU.mult).then_inc(s_rw, 1)

            def finish(j, k):
                wait(dve, s_r3, j + 1)
                dve.tensor_tensor(tok_x[:, k, :], tok_x[:, k, :], ps[:, 2 + k, :], ALU.add).then_inc(s_r4, 1)

            in_pairs(dve, TT, weigh, finish)

        @block.tensor
        def _(pe):
            pe.wait_ge(s_prep, 9)
            pe.wait_ge(s_const, NCONST)
            pe.transpose(ps[:, 2, 0:NU], par[:, 7, :], ident[0:NU, 0:NU])
            pe.transpose(ps[:, 2, NU:2 * NU], par[:, 4, :], ident[0:NU, 0:NU]).then_inc(s_tr, 1)
            pe.wait_ge(s_rt, 16)
            pe.matmul(ps[:, 3, 0:E], tri, small[:, 0, :], start=True, stop=True)
            pe.matmul(ps[:, 3, E:2 * E], ones, small[:, 0, :], start=True, stop=True).then_inc(s_rp, 1)
            pe.wait_ge(s_prep, 12)
            pe.wait_ge(s_om, 16)

            def table(i):
                wait(pe, s_cp, i)
                for k in range(2):
                    u = 2 * i + k
                    wait(pe, s_exp, u + 1)
                    col = u if isinstance(u, int) else pe.snap(u)
                    o0 = u * UC if isinstance(u, int) else pe.snap(u * UC)
                    pe.matmul(ps[:, 0, k * UC:(k + 1) * UC], decay[:, k, :],
                              coef8[:, bass.ds(col, 1), :].rearrange("p a b -> p (a b)"),
                              start=True, stop=False, skip_group_check=True)
                    pe.matmul(ps[:, 0, k * UC:(k + 1) * UC], last[:], om[:, bass.ds(o0, UC)],
                              start=False, stop=True, skip_group_check=True)
                    ins = pe.transpose(ps[:, 1, k * P:(k + 1) * P], decay[:, k, :], ident[:])
                ins.then_inc(s_tap, 1)

            table(0)
            with pe.Fori(1, NK) as i:
                table(i)
            pe.wait_ge(s_cp, NK)

            def local(i, k):
                u = 2 * i + k
                wait(pe, s_xn, u + 1)
                wait(pe, s_raw, u + 1)
                if k == 0:
                    wait(pe, s_w, 32 * (i + 1))
                h = i % 2
                if not isinstance(i, int):
                    h = pe.snap(h)
                w = wb[:, bass.ds(h, 1)].rearrange("p h m d -> p (h m) d")
                for b, (a, z) in enumerate(BANKS):
                    wait(pe, s_ev, 3 * (u - 2) + b + 1)
                    for d in range(a, z):
                        o = ps[:, 3 * k + b, NI * (d - a):NI * (d - a + 1)]
                        pe.matmul(o[:, 0:P], raw[:, k, d, :], ident[:], start=(d == a), stop=False,
                                  is_transpose=True, skip_group_check=True)
                    for d in range(a, z):
                        o = ps[:, 3 * k + b, NI * (d - a):NI * (d - a + 1)]
                        c = k * UC + d
                        ins = pe.matmul(o[:, ::-1], xn[:, k, d, :], w[:, :, c:c + 1].rearrange("p m d -> p (m d)"),
                                        start=False, stop=(d == z - 1), skip_group_check=True)
                ins.then_inc(s_loc, 1)

            def between(i, k):
                u = 2 * i + k
                wait(pe, s_st, u + 1)
                for b, (a, z) in enumerate(BANKS):
                    o = ps[:, 3 * k + b, 0:NI * (z - a)].rearrange("p (d m) -> p d m", m=NI)[:, :, 0:P]
                    pe.matmul(o, state[:, k, :], carry[:, k, a * P:z * P].rearrange("p (d t) -> p d t", t=P),
                              start=False, stop=True, skip_group_check=True).then_inc(s_pe, 1)

            def steps(i, first, final):
                for k in range(2):
                    u = 2 * i + k
                    local(i, k)
                    if not (first and k == 0):
                        between(i if k == 1 else i - 1, 1 - k)
                    wait(pe, s_cs, 2 * (u + 1))
                    pe.transpose(ps[:, 6 + k, 0:P], chunk_s[:, k, :], ident[:]).then_inc(s_tr, 1)

            over_blocks(pe, steps)
            between(NB - 1, 1)

            pe.wait_ge(s_ev, 3 * UT * NT)
            pe.wait_ge(s_wl, 48)
            for c in range(KC + FC):
                wait(pe, s_wc, c - 1)
                for m in range(KC):
                    src = load1a[:, m, c * P:(c + 1) * P] if c < KC else load2a[:, m, (c - KC) * P:(c - KC + 1) * P]
                    ins = pe.transpose(ps[:, c % 2, m * P:(m + 1) * P], src, ident[:])
                ins.then_inc(s_wt, 1)
            pe.wait_ge(s_sf, 1)
            pe.transpose(ps[:, 4, 0:RT], slots_f, ident[0:RT, 0:RT]).then_inc(s_sf, 1)
            pe.wait_ge(s_wc, KC + FC)

            def turn(j, k, s_in, s_done):
                wait(pe, s_in, j + 1)
                for c in range(KC):
                    ins = pe.transpose(ps[:, k, c * P:(c + 1) * P], tok_n[:, k, c * P:(c + 1) * P], ident[:])
                ins.then_inc(s_done, 1)

            def product(j, k, w, s_in, s_freed, s_done):
                wait(pe, s_in, j + 1)
                wait(pe, s_freed, j - 1)
                for c in range(KC):
                    ins = pe.matmul(ps[:, 2 + k, :], tok_t[:, k, c * P:(c + 1) * P], w[:, c, :],
                                    start=(c == 0), stop=(c == KC - 1))
                ins.then_inc(s_done, 1)

            def token_tiles(w, s_in, s_turned, s_copied, s_freed, s_done):
                in_pairs(pe, TT, lambda j, k: turn(j, k, s_in, s_turned),
                         lambda j, k: product(j, k, w, s_copied, s_freed, s_done))

            token_tiles(w1at, s_tn, s_tt, s_tc, s_tb, s_ta)
            pe.wait_ge(s_tc, TT)

            def turn_route(t, k):
                hold(pe, s_g[k], 16 * (t // 2 + 1), s_const)
                pe.transpose(ps[0:RANK, 6 + k, 0:P], route_a[:, k, :], ident[:]).then_inc(s_gt, 1)

            def up(t, k):
                wait(pe, s_gc, t + 1)
                wait(pe, s_wu[k], 16 * (t // 2 + 1))
                for b in range(4):
                    wait(pe, s_ge, 4 * (t - 1) + b + 1)
                    for f in range(FC // 4):
                        c = b * (FC // 4) + f
                        ins = pe.matmul(ps[:, b, f * P:(f + 1) * P], w1bs[:, k, c * P:(c + 1) * P],
                                        route_t[0:RANK, k, :], start=True, stop=True)
                    ins.then_inc(s_up, 1)

            def down(t, k):
                tt = t if isinstance(t, int) else pe.snap(t)
                e = pe.value_load(t_e[0:1, bass.ds(tt, 1)], min_val=0, max_val=E - 1)
                col = pe.snap(e * RANK)
                wait(pe, s_y, t - 1)
                for c in range(FC):
                    if c % (FC // 4) == 0:
                        wait(pe, s_ge, 4 * t + c // (FC // 4) + 1)
                    ins = pe.matmul(ps[:, 4 + k, 0:RANK], act_h[k][:, c, :], w2at[:, c, bass.ds(col, RANK)],
                                    start=(c == 0), stop=(c == FC - 1))
                ins.then_inc(s_dn, 1)

            turn_route(0, 0)
            up(0, 0)
            turn_route(1, 1)
            up(1, 1)
            turn_route(2, 0)
            down(0, 0)
            up(2, 0)
            turn_route(3, 1)
            down(1, 1)

            def route(t, k):
                up(t, k)
                turn_route(t + 1, 1 - k)
                down(t - 1, 1 - k)

            with pe.Fori(1, RT // 2 - 1) as q:
                route(q * 2 + 1, 1)
                route(q * 2 + 2, 0)
            up(RT - 1, 1)
            down(RT - 2, 0)
            down(RT - 1, 1)
            token_tiles(w2bs, s_rw, s_r1, s_r2, s_r4, s_r3)


_INS = ["L0_attn_x", "L0_attn_delta", "L0_attn_alpha", "L0_attn_beta", "L0_attn_gamma", "L0_attn_omega",
        "L0_ffn_expert_weights", "L0_ffn_expert_indices", "L0_ffn_w1_A", "L0_ffn_w1_B", "L0_ffn_w2_A",
        "L0_ffn_w2_B"]


def kernel(**inputs):
    import numpy as _np
    import concourse.bacc as _bacc
    from concourse import mybir as _mybir
    from concourse.bass_utils import run_bass_kernel_spmd as _run

    nc = _bacc.Bacc("TRN2", target_bir_lowering=False, num_devices=1)
    arrays, args = {}, []
    for name in _INS:
        a = _np.ascontiguousarray(inputs[name])
        arrays[name] = a
        args.append(nc.dram_tensor(name, a.shape, _mybir.dt.from_np(a.dtype), kind="ExternalInput").ap())
    shape = inputs["L0_attn_x"].shape
    args.append(nc.dram_tensor("out", shape, F32, kind="ExternalOutput").ap())
    build(nc, *args)
    r = _run(nc, [arrays], core_ids=[0])
    return r.results[0]["out"]
```

```python
from contextlib import ExitStack

import concourse.bass as bass
from concourse import mybir

F32 = mybir.dt.float32
I32 = mybir.dt.int32
ALU = mybir.AluOpType
ACT = mybir.ActivationFunctionType
AX_X = mybir.AxisListType.X

P = 128
FAR = 1e36
TINY = 1e-30
EPS = 1e-5


def wait(eng, sem, value):
    if isinstance(value, int) and value <= 0:
        return
    eng.wait_ge(sem, value)


def now(eng, *values):
    for v in values:
        if not isinstance(v, int):
            eng.compute_val(v)


def hold(eng, sem, value, met):
    now(eng, value)
    eng.wait_ge(met, 1)
    wait(eng, sem, value)


def build(nc, x, delta, alpha, beta, gamma, omega, ew, ei, w1a, w1b, w2a, w2b, out, ei_experts=8):
    B, L, D = x.shape
    N = gamma.shape[1]
    CH = L // P
    HB = P // CH
    NH = B // HB
    DG = D // P
    R = B * CH
    UC = P // N
    NU = D // UC
    UT = P // UC
    KD = 2 * UC
    NK = D // KD
    BT = UT // 2
    NT = NH * DG
    NB = NT * BT
    NI = P + N
    BANKS = [(0, 3), (3, 6), (6, 8)]
    LR = 8
    LBUF = 4
    PIECES = 8
    PR = P // PIECES
    WL = 5
    NL = R // LR
    assert UC == 8 and NH == 2 and HB * NH == B and NL % LBUF == 0

    E = ei_experts
    RANK = w1a.shape[0] // E
    T = ei.shape[0]
    TK = ei.shape[1]
    FF = w1b.shape[1]
    ER = E * RANK
    KC = D // P
    FC = FF // P
    TT = T // P
    RT = (T * TK + E * (P - 1)) // P
    RT += RT % 2
    NOWHERE = 1 << 20
    assert TK * TT == NB
    assert T <= L and ER == D and RANK == 64 and TK == 2 and TT % 2 == 0 and FC % 4 == 0

    x_rows = x.rearrange("b (c s) d -> s (b c) d", s=P)
    o_rows = out.rearrange("b (c t) d -> (b c) t d", t=P)

    ctx = ExitStack()
    with ctx:
        def sb(name, shape, dt=F32):
            return ctx.enter_context(nc.sbuf_tensor(name, shape, dt))

        def sem(name):
            return ctx.enter_context(nc.semaphore(name))

        taps_d = nc.dram_tensor("taps_d", [NK, 2 * P, KD], F32).ap()
        decay_d = nc.dram_tensor("decay_d", [NK, P, N, KD], F32).ap()

        a_d = nc.dram_tensor("a_d", [T, ER], F32).ap()
        r_d = nc.dram_tensor("r_d", [T, ER], F32).ap()
        slot_d = nc.dram_tensor("slot_d", [RT, P], I32).ap()

        xb = sb("xb", [P, 2, P, P])
        wb = sb("wb", [P, 2, NI, KD])
        raw = sb("raw", [P, 2, UC, P])
        cen = sb("cen", [P, 2, UC, P])
        xn = sb("xn", [P, 2, UC, P])
        far = sb("far", [P, (UC + 1) * P])
        carry = sb("carry", [P, 2, (UC + 1) * P])
        chunk_s = sb("chunk_s", [P, 2, P])
        shift_s = sb("shift_s", [P, 2, HB, CH])
        state = sb("state", [P, 2, P])
        mean = sb("mean", [P, R])
        var = sb("var", [P, R])
        rstd = sb("rstd", [P, R])
        rate = sb("rate", [P, NU])
        coef = sb("coef", [P, NU])
        ident = sb("ident", [P, P])
        own = sb("own", [P, UC])
        back = sb("back", [P, P])
        decay = sb("decay", [P, 2, P])
        last = sb("last", [1, P])
        om = sb("om", [1, D])
        eps = sb("eps", [P, 1])

        raw_row = raw[:].rearrange("p k d r -> p (k d r)")
        cen_row = cen[:].rearrange("p k d r -> p (k d r)")
        xn_row = xn[:].rearrange("p k d r -> p (k d r)")
        stats = raw_row[:, 0:R * 6].rearrange("p (r f) -> p r f", f=6)
        par = cen_row[0:NU, 0:8 * P].rearrange("p (a b) -> p a b", a=8)
        taps = cen_row[:, 8 * P:8 * P + D].rearrange("p (k d) -> p k d", k=NK)
        zero = cen_row[:, 12 * P:12 * P + D].rearrange("p (k d) -> p k d", k=NK)
        coef8 = xn_row[:, 0:D].rearrange("p (u d) -> p u d", u=NU)
        loadbuf = xb[:, 0].rearrange("p a b -> p (a b)").rearrange("p (k r d) -> p k r d", k=LBUF, r=LR)
        decays = xb[:, 1].rearrange("p a b -> p (a b)")[:, 0:D * N].rearrange("p (k n d) -> p k n d", k=NK, n=N)

        xb_all = xb[:].rearrange("p h a b -> p (h a b)")
        wb_row = wb[:].rearrange("p h m d -> p (h m d)")
        load1a = xb_all[:, 0:KC * D].rearrange("p (m d) -> p m d", m=KC)
        load2a = xb_all[:, KC * D:KC * D + KC * FF].rearrange("p (m f) -> p m f", m=KC)
        o = KC * D + KC * FF
        WR = ER + P - RANK
        w2at = xb_all[:, o:o + FC * WR].rearrange("p (f r) -> p f r", f=FC)
        o += FC * WR
        w1at = xb_all[:, o:o + KC * ER].rearrange("p (k r) -> p k r", k=KC)
        o += KC * ER
        w2bs = xb_all[:, o:o + KC * D].rearrange("p (k d) -> p k d", k=KC)
        o += KC * D
        w1bs = xb_all[0:RANK, o:o + 2 * FF].rearrange("p (k f) -> p k f", k=2)
        assert o + 2 * FF <= 2 * P * P - P
        act_h = [raw_row.rearrange("p (f r) -> p f r", f=FC), cen_row.rearrange("p (f r) -> p f r", f=FC)]
        tok_x = xn_row[:, 0:2 * D].rearrange("p (k d) -> p k d", k=2)
        tok_o = raw_row[:, 0:2 * D].rearrange("p (k d) -> p k d", k=2)
        tok_n = xn_row[:, 2 * D:4 * D].rearrange("p (k d) -> p k d", k=2)
        tok_t = wb_row[:, 0:2 * D].rearrange("p (k d) -> p k d", k=2)
        tok_a = wb_row[:, 2 * D:4 * D].rearrange("p (k d) -> p k d", k=2)
        zeros_f = carry[:].rearrange("p k c -> p (k c)")[:, 0:4 * D]
        route_a = chunk_s[:, :, 0:RANK]
        route_y = chunk_s[:, :, RANK:2 * RANK]
        route_t = state

        carry_row = carry[:].rearrange("p k c -> p (k c)")
        hot = carry_row[:, 0:3 * E * TT].rearrange("p (k e j) -> p k e j", k=3, e=E)
        o = 3 * E * TT
        rank_in = carry_row[:, o:o + E * TT].rearrange("p (e j) -> p e j", e=E)
        o += E * TT
        tmp_e = carry_row[:, o:o + E * TT].rearrange("p (e j) -> p e j", e=E)
        o += E * TT
        e_of = carry_row[:, o:o + E * TT].rearrange("p (e j) -> p e j", e=E)
        o += E * TT
        tri = carry_row[:, o:o + P]
        o += P
        ones = carry_row[:, o:o + P]
        t_of = xn_row[0:1, D:D + RT * E].rearrange("p (t e) -> p t e", e=E)
        t_le = xn_row[0:1, D + RT * E:D + 2 * RT * E].rearrange("p (t e) -> p t e", e=E)
        slots_f = xb_all[0:RT, 2 * P * P - P:]

        idx = sb("idx", [P, TT, TK], I32)
        wgt = sb("wgt", [P, TT, TK])
        idf = sb("idf", [P, TT, TK])
        route_w = sb("route_w", [P, E, TT])
        small = sb("small", [P, 8, E])
        smalli = sb("smalli", [P, E], I32)
        posf = sb("posf", [P, TK, TT])
        rowf = sb("rowf", [P, TK, TT])
        posi = sb("posi", [P, TK, TT], I32)
        rowi = sb("rowi", [P, TK, TT], I32)
        flag = sb("flag", [P, TT])
        tok8 = sb("tok8", [P, TT])
        t_ef = sb("t_ef", [1, RT])
        t_e = sb("t_e", [1, RT], I32)
        slots_i = sb("slots_i", [RT, P], I32)
        slots = sb("slots", [P, RT], I32)
        stage_p = sb("stage_p", [P, 1], I32)
        stage_r = sb("stage_r", [P, 1], I32)
        pick_g = sb("pick_g", [P, 2], I32)
        pick_s = sb("pick_s", [P, 2], I32)
        tstat = sb("tstat", [P, 2, 12])

        ps = ctx.enter_context(nc.psum_tensor("ps", [P, 8, 512], F32))

        s_par = sem("s_par")
        s_om = sem("s_om")
        s_const = sem("s_const")
        s_prep = sem("s_prep")
        s_tap = sem("s_tap")
        s_exp = sem("s_exp")
        s_cp = sem("s_cp")
        s_tab = sem("s_tab")
        s_load = [sem(f"s_load{k}") for k in range(LBUF)]
        s_free = sem("s_free")
        s_dv = sem("s_dv")
        s_std = sem("s_std")
        s_x = sem("s_x")
        s_w = sem("s_w")
        s_cen = sem("s_cen")
        s_raw = sem("s_raw")
        s_xn = sem("s_xn")
        s_loc = sem("s_loc")
        s_cs = sem("s_cs")
        s_tr = sem("s_tr")
        s_sh = sem("s_sh")
        s_ca = sem("s_ca")
        s_st = sem("s_st")
        s_pe = sem("s_pe")
        s_ev = sem("s_ev")
        s_out = sem("s_out")

        s_idx = sem("s_idx")
        s_rt = sem("s_rt")
        s_rp = sem("s_rp")
        s_slot0 = sem("s_slot0")
        s_stg = sem("s_stg")
        s_scat = sem("s_scat")
        s_sf = sem("s_sf")
        s_slots = sem("s_slots")
        s_wl = sem("s_wl")
        s_wt = sem("s_wt")
        s_wc = sem("s_wc")
        s_zero = sem("s_zero")
        s_zf = sem("s_zf")
        s_tx = [sem(f"s_tx{k}") for k in range(2)]
        s_tv = sem("s_tv")
        s_ts = sem("s_ts")
        s_tn = sem("s_tn")
        s_tt = sem("s_tt")
        s_tc = sem("s_tc")
        s_ta = sem("s_ta")
        s_tb = sem("s_tb")
        s_td = [sem(f"s_td{k}") for k in range(2)]
        s_ch = sem("s_ch")
        s_pg = sem("s_pg")
        s_g = [sem(f"s_g{k}") for k in range(2)]
        s_gt = sem("s_gt")
        s_gc = sem("s_gc")
        s_wu = [sem(f"s_wu{k}") for k in range(2)]
        s_up = sem("s_up")
        s_ge = sem("s_ge")
        s_dn = sem("s_dn")
        s_y = sem("s_y")
        s_pk = sem("s_pk")
        s_s = [sem(f"s_s{k}") for k in range(2)]
        s_rr = [sem(f"s_rr{k}") for k in range(2)]
        s_rx = [sem(f"s_rx{k}") for k in range(2)]
        s_rw = sem("s_rw")
        s_r1 = sem("s_r1")
        s_r2 = sem("s_r2")
        s_r3 = sem("s_r3")
        s_r4 = sem("s_r4")
        s_r5 = [sem(f"s_r5{k}") for k in range(2)]

        NCONST = 29
        NROUTE = 47
        DV_STATS = 9

        block = ctx.enter_context(nc.Block())

        def tile_half(i):
            return (i // BT) % 2

        def unit_of(i, k):
            return (i // (2 * BT)) * UT + (i % BT) * 2 + k

        def unit_cols(eng, i, k):
            v = tile_half(i) * (P * P) + (i % BT) * KD + k * UC
            return v if isinstance(v, int) else eng.snap(v)

        xb_row = xb[:].rearrange("p h a b -> p (h a) b")

        def unit_view(eng, i, k):
            row = tile_half(i) * P
            col = (i % BT) * KD + k * UC
            if not isinstance(i, int):
                row, col = eng.snap(row), eng.snap(col)
            return xb_row[:, bass.ds(row, P), bass.ds(col, UC)]

        def in_pairs(eng, n, step, later=None, lag=2):
            def pair(q):
                for k in range(2):
                    j = q * 2 + k
                    step(j, k)
                    if later is not None and not (isinstance(j, int) and j < lag):
                        later(j - lag, (k - lag) % 2)

            pair(0)
            pair(1)
            with eng.Fori(2, n // 2) as q:
                pair(q)
            if later is not None:
                for j in range(n - lag, n):
                    later(j, j % 2)

        def over_blocks(eng, step):
            step(0, True, False)
            with eng.Fori(1, NB - 1) as i:
                step(i, False, False)
            step(NB - 1, False, True)

        @block.gpsimd
        def _(pool):
            n = 0

            def const(ins):
                nonlocal n
                n += 1
                ins.then_inc(s_const, 1)
                pool.wait_ge(s_const, n)

            const(pool.memset(ident[:], 1.0))
            const(pool.affine_select(out=ident[:], in_=ident[:], compare_op=ALU.is_equal, fill=0.0,
                                     base=0, pattern=[[-1, P]], channel_multiplier=1))
            const(pool.memset(own[:], 1.0))
            const(pool.affine_select(out=own[:], in_=own[:], compare_op=ALU.is_ge, fill=0.0,
                                     base=0, pattern=[[-N, UC]], channel_multiplier=1))
            const(pool.affine_select(out=own[:], in_=own[:], compare_op=ALU.is_ge, fill=0.0,
                                     base=N - 1, pattern=[[N, UC]], channel_multiplier=-1))
            const(pool.iota(back[:], pattern=[[-1, P]], base=P - 1, channel_multiplier=0,
                            allow_small_or_imprecise_dtypes=True))
            const(pool.memset(last[:], 0.0))
            const(pool.memset(last[:, P - 1:P], 1.0))
            const(pool.memset(zero, 0.0))
            const(pool.memset(eps[:], EPS))
            const(pool.memset(wb[:], 0.0))
            cv = far[:, 0:UC * P].rearrange("p (j t) -> p j t", j=UC)
            const(pool.iota(cv, pattern=[[0, UC], [1, P]], base=1, channel_multiplier=0,
                            allow_small_or_imprecise_dtypes=True))
            const(pool.affine_select(out=cv, in_=cv, compare_op=ALU.is_ge, fill=FAR,
                                     base=0, pattern=[[-N, UC], [0, P]], channel_multiplier=1))
            const(pool.affine_select(out=cv, in_=cv, compare_op=ALU.is_ge, fill=FAR,
                                     base=N - 1, pattern=[[N, UC], [0, P]], channel_multiplier=-1))
            const(pool.memset(far[:, UC * P:], float(P)))
            const(pool.memset(far[:, UC * P:].rearrange("p (b c) -> p b c", b=HB)[:, :, 0:1], FAR))
            const(pool.memset(shift_s[:], 0.0))

            const(pool.iota(e_of, pattern=[[1, E], [0, TT]], base=0, channel_multiplier=0,
                            allow_small_or_imprecise_dtypes=True))
            const(pool.iota(tok8[:], pattern=[[E, TT]], base=0, channel_multiplier=E * TT,
                            allow_small_or_imprecise_dtypes=True))
            const(pool.memset(ones, 1.0))
            const(pool.memset(tri, 1.0))
            const(pool.affine_select(out=tri, in_=tri, compare_op=ALU.is_gt, fill=0.0,
                                     base=0, pattern=[[1, P]], channel_multiplier=-1))
            const(pool.iota(t_of, pattern=[[1, RT], [0, E]], base=0, channel_multiplier=0,
                            allow_small_or_imprecise_dtypes=True))
            const(pool.memset(slots_i[:], NOWHERE))
            const(pool.memset(pick_g[:], NOWHERE))
            const(pool.memset(pick_s[:], NOWHERE))
            const(pool.memset(stage_p[:], NOWHERE))
            const(pool.memset(stage_r[:], NOWHERE))
            const(pool.memset(t_e[:], 0))

            pool.wait_ge(s_rt, NROUTE)
            pool.wait_ge(s_slot0, 16)
            pool.wait_ge(s_dv, DV_STATS)
            pos_col = posi[:].rearrange("p k j -> p (k j)")
            row_col = rowi[:].rearrange("p k j -> p (k j)")

            def send(i):
                ii = i if isinstance(i, int) else pool.snap(i)
                wait(pool, s_scat, 16 * i)
                pool.tensor_copy(stage_p[:], pos_col[:, bass.ds(ii, 1)]).then_inc(s_stg, 1)
                pool.tensor_copy(stage_r[:], row_col[:, bass.ds(ii, 1)]).then_inc(s_stg, 1)
                hold(pool, s_stg, 2 * (i + 1), s_const)
                pool.indirect_dma_start(
                    out=slot_d.rearrange("a b -> (a b)")[:, None],
                    out_offset=bass.IndirectOffsetOnAxis(ap=stage_p[:], axis=0),
                    in_=stage_r[:], in_offset=None,
                    bounds_check=RT * P - 1, oob_is_err=False).then_inc(s_scat, 16)

            def centre(i, first, final):
                send(i)
                for k in range(2):
                    u = 2 * i + k
                    wait(pool, s_x, (i // BT + 1) * 16 * PIECES)
                    wait(pool, s_xn, u - 1)
                    h = tile_half(i) * P
                    if not isinstance(i, int):
                        h = pool.snap(h)
                    pool.tensor_tensor(cen[:, k].rearrange("p d r -> p r d"), unit_view(pool, i, k),
                                       mean[:, bass.ds(h, P)][:, :, None].to_broadcast([P, P, UC]),
                                       ALU.subtract).then_inc(s_cen, 1)

            over_blocks(pool, centre)

            for k in range(2):
                pool.wait_ge(s_td[k], 16 * (TT // 2))
            pool.wait_ge(s_sf, 3)
            pool.wait_ge(s_zero, 16 * (TT // 4))
            pool.wait_ge(s_zf, 2)

            def gather(t, k):
                tt = t if isinstance(t, int) else pool.snap(t)
                wait(pool, s_g[k], 16 * (t // 2))
                wait(pool, s_gt, t - 1)
                pool.tensor_copy(pick_g[:, k:k + 1], slots[:, bass.ds(tt, 1)]).then_inc(s_pg, 1)
                hold(pool, s_pg, t + 1, s_const)
                pool.indirect_dma_start(
                    out=route_a[:, k, :], out_offset=None, in_=a_d.rearrange("t (e r) -> (t e) r", e=E),
                    in_offset=bass.IndirectOffsetOnAxis(ap=pick_g[:, k:k + 1], axis=0),
                    bounds_check=T * E - 1, oob_is_err=False).then_inc(s_g[k], 16)

            def scatter(t, k):
                tt = t if isinstance(t, int) else pool.snap(t)
                wait(pool, s_s[k], 16 * (t // 2))
                pool.tensor_copy(pick_s[:, k:k + 1], slots[:, bass.ds(tt, 1)]).then_inc(s_pk, 1)
                hold(pool, s_pk, t + 1, s_const)
                wait(pool, s_y, t + 1)
                pool.indirect_dma_start(
                    out=r_d.rearrange("t (e r) -> (t e) r", e=E),
                    out_offset=bass.IndirectOffsetOnAxis(ap=pick_s[:, k:k + 1], axis=0),
                    in_=route_y[:, k, :], in_offset=None,
                    bounds_check=T * E - 1, oob_is_err=False).then_inc(s_s[k], 16)

            gather(0, 0)
            gather(1, 1)
            gather(2, 0)
            gather(3, 1)
            scatter(0, 0)
            gather(4, 0)
            scatter(1, 1)
            gather(5, 1)
            scatter(2, 0)
            with pool.Fori(3, RT // 2) as q:
                gather(q * 2, 0)
                scatter(q * 2 - 3, 1)
                gather(q * 2 + 1, 1)
                scatter(q * 2 - 2, 0)
            scatter(RT - 3, 1)
            scatter(RT - 2, 0)
            scatter(RT - 1, 1)

        @block.sync
        def _(sp):
            for j, a in enumerate((delta, alpha, beta)):
                sp.dma_start(par[:, j, :], a.rearrange("(u d) n o -> u (d n o)", d=UC)).then_inc(s_par, 16)
            sp.dma_start(par[:, 3, :], gamma.rearrange("(u d) n -> u (d n)", d=UC)).then_inc(s_par, 16)
            sp.dma_start(om[:], omega.rearrange("(a d) -> a d", a=1)).then_inc(s_om, 16)
            sp.dma_start(idx[:], ei.rearrange("(p j) k -> p j k", p=P)).then_inc(s_idx, 16)
            sp.dma_start(wgt[:], ew.rearrange("(p j) k -> p j k", p=P)).then_inc(s_idx, 16)
            for k in range(LBUF):
                sp.dma_start(loadbuf[:, k], x_rows[:, k * LR:(k + 1) * LR, :]).then_inc(s_load[k], 16)
            with sp.Fori(1, NL // LBUF) as q:
                for k in range(LBUF):
                    at = sp.snap(q * (LBUF * LR) + k * LR)
                    sp.wait_ge(s_free, sp.snap((q - 1) * LBUF + k + 1))
                    sp.dma_start(loadbuf[:, k], x_rows[:, bass.ds(at, LR), :])\
                        .then_inc(s_load[k], 16)
            sp.wait_ge(s_const, NCONST)
            sp.dma_start(slot_d, slots_i[:]).then_inc(s_slot0, 16)
            sp.wait_ge(s_cp, NK)
            sp.dma_start(taps_d[:, 0:P, :].rearrange("k i d -> i k d"), taps).then_inc(s_tab, 16)
            sp.dma_start(taps_d[:, P:2 * P, :].rearrange("k i d -> i k d"), zero).then_inc(s_tab, 16)
            sp.dma_start(decay_d.rearrange("k s n d -> s k (n d)"),
                         decays.rearrange("p k n d -> p k (n d)")).then_inc(s_tab, 16)
            sp.wait_ge(s_tab, 48)

            def piece(t, j):
                v = (t % 2) * P + j * PR, (t % 2) * P + j * PR, (t // 2) * P
                return [a if isinstance(a, int) else sp.snap(a) for a in v]

            def load_tile(t, pieces, after=None, value=0):
                for j in pieces:
                    r0, row, d0 = piece(t, j)
                    if after is not None:
                        wait(sp, after, value + 16 * (j + 1))
                    sp.dma_start(xb_row[:, bass.ds(r0, PR), :], x_rows[:, bass.ds(row, PR), bass.ds(d0, P)])\
                      .then_inc(s_x, 16)

            def store_tile(t, pieces):
                for j in pieces:
                    r0, _, d0 = piece(t, j)
                    p0 = (t % 2) * P
                    p0 = p0 if isinstance(p0, int) else sp.snap(p0)
                    sp.dma_start(o_rows[bass.ds(p0, P), j * PR:(j + 1) * PR, bass.ds(d0, P)],
                                 xb_row[:, bass.ds(r0, PR), :]).then_inc(s_out, 16)

            def load_weights(i):
                kb = (i // (2 * BT)) * BT + i % BT
                h = i % 2
                if not isinstance(i, int):
                    kb, h = sp.snap(kb), sp.snap(h)
                dst = wb[:, bass.ds(h, 1)].rearrange("p h m d -> p (h m) d")
                row = taps_d[bass.ds(kb, 1)].rearrange("k i d -> k (i d)")
                dec = decay_d[bass.ds(kb, 1)].rearrange("k s n d -> (k s) n d")
                loads, read = 16 * WL * i, 2 * (i - 1)
                now(sp, loads, read)
                wait(sp, s_w, loads)
                wait(sp, s_loc, read)
                for s0 in range(0, P, P // 4):
                    reach = P - s0
                    src = bass.AP(row.tensor, row.offset + s0 * KD, [[KD, P // 4], [1, reach * KD]])
                    sp.dma_start(dst[s0:s0 + P // 4, N:N + reach, :], src).then_inc(s_w, 16)
                sp.dma_start(dst[:, 0:N, :], dec).then_inc(s_w, 16)

            sp.wait_ge(s_dv, DV_STATS)
            load_tile(0, range(PIECES))

            def tile(t, first, final):
                for b in range(BT):
                    load_weights(t * BT + b)
                    if first:
                        if b == 2:
                            load_tile(1, range(PIECES))
                        continue
                    if b == 1:
                        wait(sp, s_ev, 3 * UT * t)
                    for j in range(3 * (b - 1), 3 * b):
                        if 0 <= j < PIECES:
                            store_tile(t - 1, [j])
                        elif PIECES <= j < 2 * PIECES and not final:
                            load_tile(t + 1, [j - PIECES], s_out, 16 * PIECES * (t - 1))

            tile(0, True, False)
            with sp.Fori(1, NT - 1) as t:
                tile(t, False, False)
            tile(NT - 1, False, True)
            sp.wait_ge(s_ev, 3 * UT * NT)
            store_tile(NT - 1, range(PIECES))
            sp.wait_ge(s_out, 16 * PIECES * NT)

            sp.wait_ge(s_pe, 3 * UT * NT)
            sp.dma_start(load1a, w1a.rearrange("(m p) d -> p m d", p=P)).then_inc(s_wl, 16)
            sp.dma_start(load2a, w2a.rearrange("(m p) f -> p m f", p=P)).then_inc(s_wl, 16)
            sp.dma_start(w2bs, w2b.rearrange("(k p) d -> p k d", p=P)).then_inc(s_wl, 16)
            sp.wait_ge(s_scat, 16 * NB)
            sp.dma_start(slots_i[:], slot_d).then_inc(s_slots, 16)
            sp.wait_ge(s_zf, 1)
            for q in range(TT // 4):
                sp.dma_start(r_d.rearrange("(q p a) r -> q p (a r)", p=P, a=4)[q], zeros_f).then_inc(s_zero, 16)

            x_tok = out.rearrange("b l d -> (b l) d")[0:T].rearrange("(p j) d -> j p d", j=TT)
            a_tok = a_d.rearrange("(p j) r -> j p r", j=TT)
            r_tok = r_d.rearrange("(p j) r -> j p r", j=TT)

            def one(ap, j):
                if not isinstance(j, int):
                    j = sp.snap(j)
                return ap[bass.ds(j, 1)].rearrange("a p d -> (a p) d")

            def tok_load(j, k):
                wait(sp, s_tn, j - 1)
                sp.dma_start(tok_x[:, k, :], one(x_tok, j)).then_inc(s_tx[k], 16)

            def tok_store(j, k):
                v = one(a_tok, j)
                wait(sp, s_tb, j + 1)
                sp.dma_start(v, tok_a[:, k, :]).then_inc(s_td[k], 16)

            in_pairs(sp, TT, tok_load, tok_store, lag=3)

            def up_load(t, k):
                tt = t if isinstance(t, int) else sp.snap(t)
                e = sp.value_load(t_e[0:1, bass.ds(tt, 1)], min_val=0, max_val=E - 1)
                row = sp.snap(e * RANK)
                wait(sp, s_up, 4 * (t - 1))
                sp.dma_start(w1bs[:, k, :], w1b[bass.ds(row, RANK), :]).then_inc(s_wu[k], 16)

            in_pairs(sp, RT, up_load)

            for k in range(2):
                sp.wait_ge(s_s[k], 16 * (RT // 2))

            def res_load(j, k):
                v = one(r_tok, j)
                wait(sp, s_rw, j - 1)
                sp.dma_start(tok_a[:, k, :], v).then_inc(s_rr[k], 16)
                if isinstance(j, int) and j < 2:
                    sp.dma_start(tok_x[:, k, :], one(x_tok, j)).then_inc(s_rx[k], 16)

            def res_store(j, k):
                v = one(x_tok, j)
                wait(sp, s_r4, j + 1)
                sp.dma_start(v, tok_o[:, k, :]).then_inc(s_r5[k], 16)
                if not (isinstance(j, int) and j >= TT - 2):
                    sp.dma_start(tok_x[:, k, :], one(x_tok, j + 2)).then_inc(s_rx[k], 16)

            in_pairs(sp, TT, res_load, res_store, lag=3)
            for k in range(2):
                sp.wait_ge(s_r5[k], 16 * (TT // 2))

        @block.scalar
        def _(act):
            act.wait_ge(s_par, 64)
            act.activation(par[:, 4, :], par[:, 0, :], ACT.Sigmoid).then_inc(s_prep, 1)
            act.activation(par[:, 5, :], par[:, 1, :], ACT.Sigmoid).then_inc(s_prep, 1)
            act.wait_ge(s_prep, 4)
            act.activation(par[:, 7, :], par[:, 6, :], ACT.Ln).then_inc(s_prep, 1)
            act.wait_ge(s_prep, 11)

            def table(i, first, final):
                for k in range(2):
                    u = 2 * i + k
                    if not first:
                        wait(act, s_tap, i)
                    col = u if isinstance(u, int) else act.snap(u)
                    act.activation(decay[:, k, :], back[:], ACT.Exp, scale=rate[:, bass.ds(col, 1)])\
                       .then_inc(s_exp, 1)
                ii = i if isinstance(i, int) else act.snap(i)
                act.wait_ge(s_tap, (i + 1) if isinstance(i, int) else act.snap(i + 1))
                act.activation(taps[:, bass.ds(ii, 1), :].rearrange("p k d -> p (k d)"), ps[:, 0, 0:KD],
                               ACT.Copy)
                for k in range(2):
                    dst = decays[:, bass.ds(ii, 1), :, k * UC:(k + 1) * UC].rearrange("p k n d -> p (k n) d")
                    ins = act.activation(dst.rearrange("p n d -> p d n"),
                                         ps[:, 1, k * P:(k + 1) * P].rearrange("p (d n) -> p d n", d=UC)[:, :, ::-1],
                                         ACT.Copy)
                ins.then_inc(s_cp, 1)

            act.wait_ge(s_const, NCONST)
            table(0, True, False)
            with act.Fori(1, NK) as i:
                table(i, False, False)
            act.wait_ge(s_dv, DV_STATS - 1)
            act.activation(rstd[:], var[:], ACT.Sqrt, bias=eps[:, 0:1]).then_inc(s_std, 1)

            def evacuate(i, k):
                u = 2 * i + k
                view = unit_view(act, i, k)
                for b, (a, z) in enumerate(BANKS):
                    wait(act, s_pe, 3 * u + b + 1)
                    act.activation(view[:, :, a:z].rearrange("p t d -> p d t"),
                                   ps[:, 3 * k + b, 0:NI * (z - a)].rearrange("p (d t) -> p d t", t=NI)[:, :, 0:P],
                                   ACT.Copy).then_inc(s_ev, 1)

            def steps(i, first, final):
                for k in range(2):
                    u = 2 * i + k
                    col = unit_of(i, k)
                    if not isinstance(i, int):
                        col = act.snap(col)
                    wait(act, s_pe, 3 * (u - 1))
                    act.activation(carry[:, k, :], far[:], ACT.Exp, scale=rate[:, bass.ds(col, 1)])\
                       .then_inc(s_ca, 1)
                    if not (first and k == 0):
                        evacuate(i if k == 1 else i - 1, 1 - k)
                    wait(act, s_tr, u + 2)
                    wait(act, s_st, u - 1)
                    act.activation(shift_s[:, k, :, 1:CH],
                                   ps[:, 6 + k, 0:P].rearrange("p (b c) -> p b c", b=HB)[:, :, 0:CH - 1],
                                   ACT.Copy, scale=coef[:, bass.ds(col, 1)]).then_inc(s_sh, 1)

            over_blocks(act, steps)
            evacuate(NB - 1, 1)

            for c in range(KC + FC):
                dst = w1at[:, c, :] if c < KC else w2at[:, c - KC, 0:ER]
                act.wait_ge(s_wt, c + 1)
                act.activation(dst, ps[:, c % 2, :], ACT.Copy).then_inc(s_wc, 1)

            def deviation(j, k):
                wait(act, s_tv, j + 1)
                act.activation(tstat[:, k, 8:9], tstat[:, k, 7:8], ACT.Sqrt, bias=eps[:, 0:1]).then_inc(s_ts, 1)

            def turned(j, k):
                wait(act, s_tt, j + 1)
                act.activation(tok_t[:, k, :], ps[:, k, :], ACT.Copy).then_inc(s_tc, 1)

            in_pairs(act, TT, deviation, turned, lag=1)

            def gelus(t, k):
                for b in range(4):
                    wait(act, s_up, 4 * t + b + 1)
                    if b == 0:
                        wait(act, s_dn, t - 1)
                    n4 = FC // 4
                    act.activation(act_h[k][:, b * n4:(b + 1) * n4, :].rearrange("p f r -> p (f r)"),
                                   ps[:, b, :], ACT.Gelu).then_inc(s_ge, 1)

            in_pairs(act, RT, gelus)

            def results(j, k):
                wait(act, s_r1, j + 1)
                act.activation(tok_t[:, k, :], ps[:, k, :], ACT.Copy).then_inc(s_r2, 1)

            in_pairs(act, TT, results)

        @block.vector
        def _(dve):
            dve.wait_ge(s_prep, 2)
            dve.tensor_tensor(par[:, 6, :], par[:, 4, :], par[:, 5, :], ALU.mult).then_inc(s_prep, 1)
            dve.wait_ge(s_prep, 3)
            dve.tensor_scalar(par[:, 6, :], par[:, 6, :], -1.0, 1.0, ALU.mult, ALU.add).then_inc(s_prep, 1)
            dve.wait_ge(s_prep, 5)
            dve.tensor_scalar(par[:, 7, :], par[:, 7, :], -TINY, None, ALU.min).then_inc(s_prep, 1)
            dve.tensor_tensor(par[:, 4, :], par[:, 4, :], par[:, 2, :], ALU.mult).then_inc(s_prep, 1)
            dve.wait_ge(s_prep, 7)
            dve.tensor_scalar(par[:, 3, :], par[:, 3, :], (1.0 / N) ** 0.5, None, ALU.mult).then_inc(s_prep, 1)
            dve.wait_ge(s_prep, 8)
            dve.tensor_tensor(par[:, 4, :], par[:, 4, :], par[:, 3, :], ALU.mult).then_inc(s_prep, 1)
            dve.wait_ge(s_tr, 1)
            dve.tensor_copy(rate[:], ps[:, 2, 0:NU]).then_inc(s_prep, 1)
            dve.tensor_copy(coef[:], ps[:, 2, NU:2 * NU]).then_inc(s_prep, 1)
            dve.wait_ge(s_prep, 11)
            dve.wait_ge(s_const, NCONST)
            dve.tensor_tensor(coef8, coef[:][:, :, None].to_broadcast([P, NU, UC]),
                              own[:][:, None, :].to_broadcast([P, NU, UC]), ALU.mult).then_inc(s_prep, 1)

            n = 0

            def rt(ins):
                nonlocal n
                n += 1
                ins.then_inc(s_rt, 1)
                dve.wait_ge(s_rt, n)

            def over_e(ap):
                return ap[:, :, None].to_broadcast([P, E, TT])

            def over_t(ap):
                return ap[:, None, :].to_broadcast([P, E, TT])

            dve.wait_ge(s_idx, 32)
            rt(dve.tensor_copy(idf[:], idx[:]))
            for k in range(TK):
                rt(dve.tensor_tensor(hot[:, k], over_t(idf[:, :, k]), e_of, ALU.is_equal))
            rt(dve.tensor_tensor(hot[:, 2], hot[:, 0], hot[:, 1], ALU.max))
            rt(dve.tensor_tensor(route_w[:], hot[:, 0], over_t(wgt[:, :, 0]), ALU.mult))
            rt(dve.tensor_tensor(tmp_e, hot[:, 1], over_t(wgt[:, :, 1]), ALU.mult))
            rt(dve.tensor_tensor(route_w[:], route_w[:], tmp_e, ALU.add))
            for e in range(E):
                rt(dve.tensor_tensor_scan(rank_in[:, e, :], ones[:, 0:TT], hot[:, 2, e, :], 0.0,
                                          ALU.mult, ALU.add))
            rt(dve.tensor_copy(small[:, 0, :], rank_in[:, :, TT - 1]))
            dve.wait_ge(s_rp, 1)
            rt(dve.tensor_copy(small[:, 1, :], ps[:, 3, 0:E]))
            rt(dve.tensor_scalar(smalli[:], ps[:, 3, E:2 * E], float(P - 1), None, ALU.add))
            rt(dve.tensor_scalar(smalli[:], smalli[:], P.bit_length() - 1, None, ALU.arith_shift_right))
            rt(dve.tensor_copy(small[:, 2, :], smalli[:]))
            rt(dve.tensor_tensor_scan(small[:, 3, :], ones[:, 0:E], small[:, 2, :], 0.0, ALU.mult, ALU.add))
            rt(dve.tensor_tensor(small[:, 4, :], small[:, 3, :], small[:, 2, :], ALU.subtract))
            rt(dve.tensor_scalar(small[:, 4, :], small[:, 4, :], float(P), -1.0, ALU.mult, ALU.add))
            rt(dve.tensor_tensor(small[:, 4, :], small[:, 4, :], small[:, 1, :], ALU.add))
            rt(dve.tensor_tensor(rank_in, rank_in, over_e(small[:, 4, :]), ALU.add))
            for k in range(TK):
                rt(dve.tensor_reduce(flag[:], hot[:, k].rearrange("p e j -> p j e"), AX_X, ALU.add))
                rt(dve.tensor_scalar(flag[:], flag[:], -float(NOWHERE), float(NOWHERE), ALU.mult, ALU.add))
                rt(dve.tensor_tensor(tmp_e, hot[:, k], rank_in, ALU.mult))
                rt(dve.tensor_reduce(posf[:, k, :], tmp_e.rearrange("p e j -> p j e"), AX_X, ALU.add))
                rt(dve.tensor_tensor(posf[:, k, :], posf[:, k, :], flag[:], ALU.add))
                rt(dve.tensor_tensor(rowf[:, k, :], idf[:, :, k], tok8[:], ALU.add))
            rt(dve.tensor_tensor(tmp_e, hot[:, 0], hot[:, 1], ALU.mult))
            rt(dve.tensor_reduce(flag[:], tmp_e.rearrange("p e j -> p j e"), AX_X, ALU.add))
            rt(dve.tensor_scalar(flag[:], flag[:], float(NOWHERE), None, ALU.mult))
            rt(dve.tensor_tensor(posf[:, 1, :], posf[:, 1, :], flag[:], ALU.add))
            rt(dve.tensor_copy(posi[:], posf[:]))
            rt(dve.tensor_copy(rowi[:], rowf[:]))
            rt(dve.tensor_tensor(t_le, small[0:1, 3, :][:, None, :].to_broadcast([1, RT, E]), t_of,
                                 ALU.is_le))
            rt(dve.tensor_reduce(t_ef[:], t_le, AX_X, ALU.add))
            rt(dve.tensor_scalar(t_ef[:], t_ef[:], float(E - 1), None, ALU.min))
            rt(dve.tensor_copy(t_e[:], t_ef[:]))
            assert n == NROUTE, n

            def row_stats(q):
                for k in range(LBUF):
                    wait(dve, s_load[k], 16 * (q + 1))
                    for r in range(LR):
                        at = q * (LBUF * LR) + k * LR + r
                        if not isinstance(q, int):
                            at = dve.snap(at)
                        ins = dve.bn_stats(stats[:, bass.ds(at, 1), :].rearrange("p a b -> p (a b)"),
                                           loadbuf[:, k, r, :])
                    ins.then_inc(s_free, 1)

            row_stats(0)
            with dve.Fori(1, NL // LBUF) as q:
                row_stats(q)
            dve.wait_ge(s_free, NL)
            n = 0

            def chain(ins):
                nonlocal n
                n += 1
                ins.then_inc(s_dv, 1)
                dve.wait_ge(s_dv, n)

            st = stats.rearrange("p r f -> p f r")
            chain(dve.tensor_tensor(mean[:], st[:, 1, :], st[:, 4, :], ALU.add))
            chain(dve.tensor_scalar(mean[:], mean[:], 0.5, None, ALU.mult))
            chain(dve.tensor_tensor(rstd[:], st[:, 1, :], st[:, 4, :], ALU.subtract))
            chain(dve.tensor_tensor(rstd[:], rstd[:], rstd[:], ALU.mult))
            chain(dve.tensor_scalar(rstd[:], rstd[:], D / 4.0, None, ALU.mult))
            chain(dve.tensor_tensor(rstd[:], rstd[:], st[:, 2, :], ALU.add))
            chain(dve.tensor_tensor(rstd[:], rstd[:], st[:, 5, :], ALU.add))
            chain(dve.tensor_scalar(var[:], rstd[:], 1.0 / D, None, ALU.mult))
            dve.wait_ge(s_std, 1)
            chain(dve.reciprocal(rstd[:], rstd[:]))
            assert n == DV_STATS

            def stage(i, k):
                u = 2 * i + k
                wait(dve, s_x, (i // BT + 1) * 16 * PIECES)
                wait(dve, s_loc, u - 1)
                dve.tensor_copy(raw[:, k].rearrange("p d r -> p r d"), unit_view(dve, i, k)).then_inc(s_raw, 1)
                wait(dve, s_cen, u + 1)
                h = tile_half(i) * P
                if not isinstance(i, int):
                    h = dve.snap(h)
                dve.tensor_tensor(xn[:, k], cen[:, k],
                                  rstd[:, bass.ds(h, P)][:, None, :].to_broadcast([P, UC, P]),
                                  ALU.mult).then_inc(s_xn, 1)

            def steps(i, first, final):
                for k in range(2):
                    u = 2 * i + k
                    if not (final and k == 1):
                        stage(i if k == 0 else i + 1, 1 - k)
                    wait(dve, s_loc, u + 1)
                    wait(dve, s_tr, u)
                    dst = chunk_s[:, k, :].rearrange("p (d n) -> p d n", n=N)
                    src = ps[:, 3 * k:3 * k + 2, 0:3 * NI].rearrange("p a (d m) -> p a d m", m=NI)[:, :, :, P:]
                    dve.tensor_copy(dst[:, 0:6].rearrange("p (a d) n -> p a d n", a=2), src).then_inc(s_cs, 1)
                    src = ps[:, 3 * k + 2, 0:2 * NI].rearrange("p (d m) -> p d m", m=NI)[:, :, P:]
                    dve.tensor_copy(dst[:, 6:8], src).then_inc(s_cs, 1)
                    wait(dve, s_sh, u + 1)
                    wait(dve, s_ca, u + 1)
                    wait(dve, s_pe, 3 * (u - 1))
                    dve.tensor_tensor_scan(state[:, k, :], carry[:, k, UC * P:],
                                           shift_s[:, k].rearrange("p b c -> p (b c)"), 0.0,
                                           ALU.mult, ALU.add).then_inc(s_st, 1)

            stage(0, 0)
            over_blocks(dve, steps)

            dve.wait_ge(s_pe, 3 * UT * NT)
            dve.memset(zeros_f, 0.0).then_inc(s_zf, 1)
            dve.memset(route_a, 0.0).then_inc(s_zf, 1)
            dve.wait_ge(s_ev, 3 * UT * NT)
            dve.wait_ge(s_out, 16 * PIECES * NT)
            dve.memset(w2at[:, :, ER:], 0.0).then_inc(s_zf, 1)
            dve.wait_ge(s_slots, 16)
            dve.tensor_copy(slots_f, slots_i[:]).then_inc(s_sf, 1)
            dve.wait_ge(s_sf, 2)
            dve.tensor_copy(slots[:], ps[:, 4, 0:RT]).then_inc(s_sf, 1)

            def tokens(j, k):
                st, m = tstat[:, k, 0:6], tstat[:, k, 6:8]
                wait(dve, s_tx[k], 16 * (j // 2 + 1))
                dve.bn_stats(st, tok_x[:, k, :]).then_inc(s_ch, 1)
                hold(dve, s_ch, 2 * j + 1, s_const)
                dve.bn_aggr(m, st).then_inc(s_tv, 1)
                wait(dve, s_ts, j + 1)
                dve.reciprocal(tstat[:, k, 9:10], tstat[:, k, 8:9]).then_inc(s_ch, 1)
                wait(dve, s_ch, 2 * j + 2)
                wait(dve, s_tt, j - 1)
                dve.tensor_scalar(tok_n[:, k, :], tok_x[:, k, :], tstat[:, k, 6:7], tstat[:, k, 9:10],
                                  ALU.subtract, ALU.mult).then_inc(s_tn, 1)

            def ranks(j, k):
                wait(dve, s_ta, j + 1)
                wait(dve, s_td[k], 16 * (j // 2))
                dve.tensor_copy(tok_a[:, k, :], ps[:, 2 + k, :]).then_inc(s_tb, 1)

            in_pairs(dve, TT, tokens, ranks)

            def routes_in(t, k):
                wait(dve, s_gt, t + 1)
                wait(dve, s_up, 4 * (t - 1))
                dve.tensor_copy(route_t[0:RANK, k, :], ps[0:RANK, 6 + k, 0:P]).then_inc(s_gc, 1)

            def routes_out(t, k):
                wait(dve, s_dn, t + 1)
                wait(dve, s_s[k], 16 * (t // 2))
                dve.tensor_copy(route_y[:, k, :], ps[:, 4 + k, 0:RANK]).then_inc(s_y, 1)

            routes_in(0, 0)
            routes_in(1, 1)
            routes_in(2, 0)
            routes_out(0, 0)
            routes_in(3, 1)
            routes_out(1, 1)
            with dve.Fori(2, RT // 2) as q:
                for k in range(2):
                    routes_in(q * 2 + k, k)
                    routes_out(q * 2 - 2 + k, k)
            routes_out(RT - 2, 0)
            routes_out(RT - 1, 1)

            def weigh(j, k):
                jj = j if isinstance(j, int) else dve.snap(j)
                wait(dve, s_rr[k], 16 * (j // 2 + 1))
                wait(dve, s_r1, j - 1)
                dve.tensor_tensor(tok_n[:, k, :].rearrange("p (e r) -> p e r", e=E),
                                  tok_a[:, k, :].rearrange("p (e r) -> p e r", e=E),
                                  route_w[:, :, bass.ds(jj, 1)].to_broadcast([P, E, RANK]),
                                  ALU.mult).then_inc(s_rw, 1)

            def finish(j, k):
                wait(dve, s_rx[k], 16 * (j // 2 + 1))
                wait(dve, s_r3, j + 1)
                wait(dve, s_r5[k], 16 * (j // 2))
                dve.tensor_tensor(tok_o[:, k, :], tok_x[:, k, :], ps[:, 2 + k, :], ALU.add).then_inc(s_r4, 1)

            in_pairs(dve, TT, weigh, finish)

        @block.tensor
        def _(pe):
            pe.wait_ge(s_prep, 9)
            pe.wait_ge(s_const, NCONST)
            pe.transpose(ps[:, 2, 0:NU], par[:, 7, :], ident[0:NU, 0:NU])
            pe.transpose(ps[:, 2, NU:2 * NU], par[:, 4, :], ident[0:NU, 0:NU]).then_inc(s_tr, 1)
            pe.wait_ge(s_rt, 16)
            pe.matmul(ps[:, 3, 0:E], tri, small[:, 0, :], start=True, stop=True)
            pe.matmul(ps[:, 3, E:2 * E], ones, small[:, 0, :], start=True, stop=True).then_inc(s_rp, 1)
            pe.wait_ge(s_prep, 12)
            pe.wait_ge(s_om, 16)

            def table(i):
                wait(pe, s_cp, i)
                for k in range(2):
                    u = 2 * i + k
                    wait(pe, s_exp, u + 1)
                    col = u if isinstance(u, int) else pe.snap(u)
                    o0 = u * UC if isinstance(u, int) else pe.snap(u * UC)
                    pe.matmul(ps[:, 0, k * UC:(k + 1) * UC], decay[:, k, :],
                              coef8[:, bass.ds(col, 1), :].rearrange("p a b -> p (a b)"),
                              start=True, stop=False, skip_group_check=True)
                    pe.matmul(ps[:, 0, k * UC:(k + 1) * UC], last[:], om[:, bass.ds(o0, UC)],
                              start=False, stop=True, skip_group_check=True)
                    ins = pe.transpose(ps[:, 1, k * P:(k + 1) * P], decay[:, k, :], ident[:])
                ins.then_inc(s_tap, 1)

            table(0)
            with pe.Fori(1, NK) as i:
                table(i)
            pe.wait_ge(s_cp, NK)

            def local(i, k):
                u = 2 * i + k
                wait(pe, s_xn, u + 1)
                wait(pe, s_raw, u + 1)
                if k == 0:
                    wait(pe, s_w, 16 * WL * (i + 1))
                h = i % 2
                if not isinstance(i, int):
                    h = pe.snap(h)
                w = wb[:, bass.ds(h, 1)].rearrange("p h m d -> p (h m) d")
                for b, (a, z) in enumerate(BANKS):
                    wait(pe, s_ev, 3 * (u - 2) + b + 1)
                    for d in range(a, z):
                        o = ps[:, 3 * k + b, NI * (d - a):NI * (d - a + 1)]
                        pe.matmul(o[:, 0:P], raw[:, k, d, :], ident[:], start=(d == a), stop=False,
                                  is_transpose=True, skip_group_check=True)
                    for d in range(a, z):
                        o = ps[:, 3 * k + b, NI * (d - a):NI * (d - a + 1)]
                        c = k * UC + d
                        ins = pe.matmul(o[:, ::-1], xn[:, k, d, :], w[:, :, c:c + 1].rearrange("p m d -> p (m d)"),
                                        start=False, stop=(d == z - 1), skip_group_check=True)
                ins.then_inc(s_loc, 1)

            def between(i, k):
                u = 2 * i + k
                wait(pe, s_st, u + 1)
                for b, (a, z) in enumerate(BANKS):
                    o = ps[:, 3 * k + b, 0:NI * (z - a)].rearrange("p (d m) -> p d m", m=NI)[:, :, 0:P]
                    pe.matmul(o, state[:, k, :], carry[:, k, a * P:z * P].rearrange("p (d t) -> p d t", t=P),
                              start=False, stop=True, skip_group_check=True).then_inc(s_pe, 1)

            def steps(i, first, final):
                for k in range(2):
                    u = 2 * i + k
                    local(i, k)
                    if not (first and k == 0):
                        between(i if k == 1 else i - 1, 1 - k)
                    wait(pe, s_cs, 2 * (u + 1))
                    pe.transpose(ps[:, 6 + k, 0:P], chunk_s[:, k, :], ident[:]).then_inc(s_tr, 1)

            over_blocks(pe, steps)
            between(NB - 1, 1)

            pe.wait_ge(s_ev, 3 * UT * NT)
            pe.wait_ge(s_wl, 48)
            for c in range(KC + FC):
                wait(pe, s_wc, c - 1)
                for m in range(KC):
                    src = load1a[:, m, c * P:(c + 1) * P] if c < KC else load2a[:, m, (c - KC) * P:(c - KC + 1) * P]
                    ins = pe.transpose(ps[:, c % 2, m * P:(m + 1) * P], src, ident[:])
                ins.then_inc(s_wt, 1)
            pe.wait_ge(s_sf, 1)
            pe.transpose(ps[:, 4, 0:RT], slots_f, ident[0:RT, 0:RT]).then_inc(s_sf, 1)
            pe.wait_ge(s_wc, KC + FC)

            def turn(j, k, s_in, s_done):
                wait(pe, s_in, j + 1)
                for c in range(KC):
                    ins = pe.transpose(ps[:, k, c * P:(c + 1) * P], tok_n[:, k, c * P:(c + 1) * P], ident[:])
                ins.then_inc(s_done, 1)

            def product(j, k, w, s_in, s_freed, s_done):
                wait(pe, s_in, j + 1)
                wait(pe, s_freed, j - 1)
                for c in range(KC):
                    ins = pe.matmul(ps[:, 2 + k, :], tok_t[:, k, c * P:(c + 1) * P], w[:, c, :],
                                    start=(c == 0), stop=(c == KC - 1))
                ins.then_inc(s_done, 1)

            def token_tiles(w, s_in, s_turned, s_copied, s_freed, s_done):
                in_pairs(pe, TT, lambda j, k: turn(j, k, s_in, s_turned),
                         lambda j, k: product(j, k, w, s_copied, s_freed, s_done), lag=1)

            token_tiles(w1at, s_tn, s_tt, s_tc, s_tb, s_ta)
            pe.wait_ge(s_tc, TT)
            pe.wait_ge(s_zf, 3)

            def turn_route(t, k):
                hold(pe, s_g[k], 16 * (t // 2 + 1), s_const)
                pe.transpose(ps[0:RANK, 6 + k, 0:P], route_a[:, k, :], ident[:]).then_inc(s_gt, 1)

            def up(t, k):
                wait(pe, s_gc, t + 1)
                wait(pe, s_wu[k], 16 * (t // 2 + 1))
                for b in range(4):
                    wait(pe, s_ge, 4 * (t - 1) + b + 1)
                    for f in range(FC // 4):
                        c = b * (FC // 4) + f
                        ins = pe.matmul(ps[:, b, f * P:(f + 1) * P], w1bs[:, k, c * P:(c + 1) * P],
                                        route_t[0:RANK, k, :], start=True, stop=True)
                    ins.then_inc(s_up, 1)

            def down(t, k):
                tt = t if isinstance(t, int) else pe.snap(t)
                e = pe.value_load(t_e[0:1, bass.ds(tt, 1)], min_val=0, max_val=E - 1)
                col = pe.snap(e * RANK)
                wait(pe, s_y, t - 1)
                for c in range(FC):
                    if c % (FC // 4) == 0:
                        wait(pe, s_ge, 4 * t + c // (FC // 4) + 1)
                    ins = pe.matmul(ps[:, 4 + k, 0:P], act_h[k][:, c, :], w2at[:, c, bass.ds(col, P)],
                                    start=(c == 0), stop=(c == FC - 1))
                ins.then_inc(s_dn, 1)

            turn_route(0, 0)
            up(0, 0)
            turn_route(1, 1)
            up(1, 1)
            turn_route(2, 0)
            down(0, 0)
            up(2, 0)
            turn_route(3, 1)
            down(1, 1)

            def route(t, k):
                up(t, k)
                turn_route(t + 1, 1 - k)
                down(t - 1, 1 - k)

            with pe.Fori(1, RT // 2 - 1) as q:
                route(q * 2 + 1, 1)
                route(q * 2 + 2, 0)
            up(RT - 1, 1)
            down(RT - 2, 0)
            down(RT - 1, 1)
            token_tiles(w2bs, s_rw, s_r1, s_r2, s_r4, s_r3)


_INS = ["L0_attn_x", "L0_attn_delta", "L0_attn_alpha", "L0_attn_beta", "L0_attn_gamma", "L0_attn_omega",
        "L0_ffn_expert_weights", "L0_ffn_expert_indices", "L0_ffn_w1_A", "L0_ffn_w1_B", "L0_ffn_w2_A",
        "L0_ffn_w2_B"]


def kernel(**inputs):
    import numpy as _np
    import concourse.bacc as _bacc
    from concourse import mybir as _mybir
    from concourse.bass_utils import run_bass_kernel_spmd as _run

    nc = _bacc.Bacc("TRN2", target_bir_lowering=False, num_devices=1)
    arrays, args = {}, []
    for name in _INS:
        a = _np.ascontiguousarray(inputs[name])
        arrays[name] = a
        args.append(nc.dram_tensor(name, a.shape, _mybir.dt.from_np(a.dtype), kind="ExternalInput").ap())
    shape = inputs["L0_attn_x"].shape
    args.append(nc.dram_tensor("out", shape, F32, kind="ExternalOutput").ap())
    build(nc, *args)
    r = _run(nc, [arrays], core_ids=[0])
    return r.results[0]["out"]
```

```python
from contextlib import ExitStack

import concourse.bass as bass
from concourse import mybir

F32 = mybir.dt.float32
I32 = mybir.dt.int32
ALU = mybir.AluOpType
ACT = mybir.ActivationFunctionType
AX_X = mybir.AxisListType.X

P = 128
FAR = 1e36
TINY = 1e-30
EPS = 1e-5


def wait(eng, sem, value):
    if isinstance(value, int) and value <= 0:
        return
    eng.wait_ge(sem, value)


def now(eng, *values):
    for v in values:
        if not isinstance(v, int):
            eng.compute_val(v)


def hold(eng, sem, value, met):
    now(eng, value)
    eng.wait_ge(met, 1)
    wait(eng, sem, value)


def build(nc, x, delta, alpha, beta, gamma, omega, ew, ei, w1a, w1b, w2a, w2b, out, ei_experts=8):
    B, L, D = x.shape
    N = gamma.shape[1]
    CH = L // P
    HB = P // CH
    NH = B // HB
    DG = D // P
    R = B * CH
    UC = P // N
    NU = D // UC
    UT = P // UC
    KD = 2 * UC
    NK = D // KD
    BT = UT // 2
    NT = NH * DG
    NB = NT * BT
    NI = P + N
    BANKS = [(0, 3), (3, 6), (6, 8)]
    LR = 4
    LBUF = 4
    NL = P // LR
    LR2 = 2
    NL2 = P // LR2
    PIECES = 16
    PR = P // PIECES
    WL = 5
    ZR = P // 4
    assert UC == 8 and NH == 2 and HB * NH == B and NL % LBUF == 0

    E = ei_experts
    RANK = w1a.shape[0] // E
    T = ei.shape[0]
    TK = ei.shape[1]
    FF = w1b.shape[1]
    ER = E * RANK
    KC = D // P
    FC = FF // P
    TT = T // P
    RT = (T * TK + E * (P - 1)) // P
    RT += RT % 2
    NOWHERE = 1 << 20
    assert T == L and PIECES % 4 == 0
    assert TK * TT == 2 * NK
    assert RT // 2 - 4 >= NL2 // 2 and TT * 4 == P and T <= HB * L
    assert T <= L and ER == D and RANK == 64 and TK == 2 and TT % 2 == 0 and FC % 4 == 0

    x_rows = x.rearrange("b (c s) d -> s (b c) d", s=P)
    o_rows = out.rearrange("b (c t) d -> (b c) t d", t=P)

    ctx = ExitStack()
    with ctx:
        def sb(name, shape, dt=F32):
            return ctx.enter_context(nc.sbuf_tensor(name, shape, dt))

        def sem(name):
            return ctx.enter_context(nc.semaphore(name))

        taps_d = nc.dram_tensor("taps_d", [NK, P + ZR, KD], F32).ap()
        decay_d = nc.dram_tensor("decay_d", [NK, P, N, KD], F32).ap()

        a_d = nc.dram_tensor("a_d", [T, ER], F32).ap()
        r_d = nc.dram_tensor("r_d", [T, ER], F32).ap()
        slot_d = nc.dram_tensor("slot_d", [RT, P], I32).ap()

        xb = sb("xb", [P, 2, P, P])
        wb = sb("wb", [P, 2, NI, KD])
        raw = sb("raw", [P, 2, UC, P])
        cen = sb("cen", [P, 2, UC, P])
        xn = sb("xn", [P, 2, UC, P])
        far = sb("far", [P, (UC + 1) * P])
        carry = sb("carry", [P, 2, (UC + 1) * P])
        chunk_s = sb("chunk_s", [P, 2, P])
        shift_s = sb("shift_s", [P, 2, HB, CH])
        state = sb("state", [P, 2, P])
        mean = sb("mean", [P, R])
        var = sb("var", [P, R])
        rstd = sb("rstd", [P, R])
        rate = sb("rate", [P, NU])
        coef = sb("coef", [P, NU])
        ident = sb("ident", [P, P])
        own = sb("own", [P, UC])
        back = sb("back", [P, P])
        decay = sb("decay", [P, 4, P])
        last = sb("last", [1, P])
        om = sb("om", [1, D])
        eps = sb("eps", [P, 1])

        raw_row = raw[:].rearrange("p k d r -> p (k d r)")
        cen_row = cen[:].rearrange("p k d r -> p (k d r)")
        xn_row = xn[:].rearrange("p k d r -> p (k d r)")
        par = cen_row[0:NU, 0:8 * P].rearrange("p (a b) -> p a b", a=8)
        taps = cen_row[:, 8 * P:8 * P + D].rearrange("p (k d) -> p k d", k=NK)
        zero = cen_row[:, 12 * P:12 * P + D].rearrange("p (k d) -> p k d", k=NK)
        coef8 = xn_row[:, 0:D].rearrange("p (u d) -> p u d", u=NU)
        xb_all = xb[:].rearrange("p h a b -> p (h a b)")
        o = P * P
        decays = xb_all[:, o:o + D * N].rearrange("p (k n d) -> p k n d", k=NK, n=N)
        o += D * N
        loadbuf = xb_all[:, o:].rearrange("p (k r d) -> p k r d", k=LBUF, r=LR)

        load1a = xb_all[:, 0:KC * D].rearrange("p (m d) -> p m d", m=KC)
        o = KC * D
        load2a = xb_all[:, o:o + KC * FF].rearrange("p (m f) -> p m f", m=KC)
        o += KC * FF
        w1at = xb_all[:, o:o + KC * ER].rearrange("p (k r) -> p k r", k=KC)
        assert o + KC * ER <= P * P
        w2bs = xb_all[:, 0:KC * D].rearrange("p (k d) -> p k d", k=KC)
        o = KC * D
        res_x, res_n, res_t, res_a, res_o = (
            xb_all[:, o + 2 * D * j:o + 2 * D * (j + 1)].rearrange("p (k d) -> p k d", k=2) for j in range(5))
        o = P * P
        WR = ER + P - RANK
        w2at = xb_all[:, o:o + FC * WR].rearrange("p (f r) -> p f r", f=FC)
        o += FC * WR
        w1bs = xb_all[0:RANK, o:o + 2 * FF].rearrange("p (k f) -> p k f", k=2)
        o += 2 * FF
        ring2 = xb_all[:, o:o + 2 * LR2 * D].rearrange("p (k r d) -> p k r d", k=2, r=LR2)
        o += 2 * LR2 * D
        stats2 = xb_all[:, o:o + 6 * P].rearrange("p (r f) -> p r f", f=6)
        assert o + 6 * P <= 2 * P * P
        tok_x, tok_n = (xn_row[:, 2 * D * j:2 * D * (j + 1)].rearrange("p (k d) -> p k d", k=2) for j in range(2))
        tok_t, tok_a = (raw_row[:, 2 * D * j:2 * D * (j + 1)].rearrange("p (k d) -> p k d", k=2) for j in range(2))
        act_h = [raw_row.rearrange("p (f r) -> p f r", f=FC), cen_row.rearrange("p (f r) -> p f r", f=FC)]
        zeros_f = carry[:].rearrange("p k c -> p (k c)")[:, 0:D]
        slots_f = carry[:].rearrange("p k c -> p (k c)")[0:RT, D:D + P]
        route_a = chunk_s[:, :, 0:RANK]
        route_y = chunk_s[:, :, RANK:2 * RANK]
        route_t = state

        carry_row = carry[:].rearrange("p k c -> p (k c)")
        hot = carry_row[:, 0:3 * E * TT].rearrange("p (k e j) -> p k e j", k=3, e=E)
        o = 3 * E * TT
        rank_in = carry_row[:, o:o + E * TT].rearrange("p (e j) -> p e j", e=E)
        o += E * TT
        tmp_e = carry_row[:, o:o + E * TT].rearrange("p (e j) -> p e j", e=E)
        o += E * TT
        e_of = carry_row[:, o:o + E * TT].rearrange("p (e j) -> p e j", e=E)
        o += E * TT
        tri = carry_row[:, o:o + P]
        o += P
        ones = carry_row[:, o:o + P]
        t_of = xn_row[0:1, D:D + RT * E].rearrange("p (t e) -> p t e", e=E)
        t_le = xn_row[0:1, D + RT * E:D + 2 * RT * E].rearrange("p (t e) -> p t e", e=E)

        idx = sb("idx", [P, TT, TK], I32)
        wgt = sb("wgt", [P, TT, TK])
        idf = sb("idf", [P, TT, TK])
        route_w = sb("route_w", [P, E, TT])
        small = sb("small", [P, 8, E])
        smalli = sb("smalli", [P, E], I32)
        posf = sb("posf", [P, TK, TT])
        rowf = sb("rowf", [P, TK, TT])
        posi = sb("posi", [P, TK, TT], I32)
        rowi = sb("rowi", [P, TK, TT], I32)
        flag = sb("flag", [P, TT])
        tok8 = sb("tok8", [P, TT])
        t_ef = sb("t_ef", [1, RT])
        t_e = sb("t_e", [1, RT], I32)
        slots_i = sb("slots_i", [RT, P], I32)
        slots = sb("slots", [P, RT], I32)
        stage_p = sb("stage_p", [P, 2], I32)
        stage_r = sb("stage_r", [P, 2], I32)
        pick_g = sb("pick_g", [P, 2], I32)
        pick_s = sb("pick_s", [P, 2], I32)
        tstat = sb("tstat", [P, 2, 12])

        ps = ctx.enter_context(nc.psum_tensor("ps", [P, 8, 512], F32))

        s_par = sem("s_par")
        s_om = sem("s_om")
        s_const = sem("s_const")
        s_prep = sem("s_prep")
        s_tap = sem("s_tap")
        s_exp = sem("s_exp")
        s_cp = sem("s_cp")
        s_tab = sem("s_tab")
        s_dec = sem("s_dec")
        s_keep = sem("s_keep")
        s_load = [sem(f"s_load{k}") for k in range(LBUF)]
        s_free = sem("s_free")
        s_load2 = [sem(f"s_load2{k}") for k in range(2)]
        s_free2 = sem("s_free2")
        s_dv = sem("s_dv")
        s_std = sem("s_std")
        s_x = sem("s_x")
        s_w = sem("s_w")
        s_cen = sem("s_cen")
        s_raw = sem("s_raw")
        s_xn = sem("s_xn")
        s_loc = sem("s_loc")
        s_cs = sem("s_cs")
        s_tr = sem("s_tr")
        s_sh = sem("s_sh")
        s_ca = sem("s_ca")
        s_st = sem("s_st")
        s_pe = sem("s_pe")
        s_ev = sem("s_ev")
        s_out = sem("s_out")
        s_first = sem("s_first")

        s_idx = sem("s_idx")
        s_rt = sem("s_rt")
        s_rp = sem("s_rp")
        s_slot0 = sem("s_slot0")
        s_stg = sem("s_stg")
        s_scat = [sem(f"s_scat{k}") for k in range(2)]
        s_sf = sem("s_sf")
        s_slots = sem("s_slots")
        s_wl = sem("s_wl")
        s_wt = sem("s_wt")
        s_wc = sem("s_wc")
        s_zero = sem("s_zero")
        s_zf = sem("s_zf")
        s_tx = [sem(f"s_tx{k}") for k in range(2)]
        s_tv = sem("s_tv")
        s_ts = sem("s_ts")
        s_tn = sem("s_tn")
        s_tt = sem("s_tt")
        s_tc = sem("s_tc")
        s_ta = sem("s_ta")
        s_tb = sem("s_tb")
        s_td = [sem(f"s_td{k}") for k in range(2)]
        s_ch = sem("s_ch")
        s_pg = sem("s_pg")
        s_g = [sem(f"s_g{k}") for k in range(2)]
        s_gt = sem("s_gt")
        s_gc = sem("s_gc")
        s_wu = [sem(f"s_wu{k}") for k in range(2)]
        s_up = sem("s_up")
        s_ge = sem("s_ge")
        s_dn = sem("s_dn")
        s_y = sem("s_y")
        s_pk = sem("s_pk")
        s_s = [sem(f"s_s{k}") for k in range(2)]
        s_rr = [sem(f"s_rr{k}") for k in range(2)]
        s_rx = [sem(f"s_rx{k}") for k in range(2)]
        s_rw = sem("s_rw")
        s_r1 = sem("s_r1")
        s_r2 = sem("s_r2")
        s_r3 = sem("s_r3")
        s_r4 = sem("s_r4")
        s_r5 = [sem(f"s_r5{k}") for k in range(2)]

        NCONST = 29
        NROUTE = 47
        QS = 2 + NL2 // 2
        DV_STATS = 9

        block = ctx.enter_context(nc.Block())

        def tile_half(i):
            return (i // BT) % 2

        xb_row = xb[:].rearrange("p h a b -> p (h a) b")

        def unit_view(eng, i, k):
            row = tile_half(i) * P
            col = (i % BT) * KD + k * UC
            if not isinstance(i, int):
                row, col = eng.snap(row), eng.snap(col)
            return xb_row[:, bass.ds(row, P), bass.ds(col, UC)]

        def in_pairs(eng, n, step, later=None, lag=2):
            def pair(q):
                for k in range(2):
                    j = q * 2 + k
                    step(j, k)
                    if later is not None and not (isinstance(j, int) and j < lag):
                        later(j - lag, (k - lag) % 2)

            pair(0)
            pair(1)
            with eng.Fori(2, n // 2) as q:
                pair(q)
            if later is not None:
                for j in range(n - lag, n):
                    later(j, j % 2)

        def over_blocks(eng, g, step):
            step(g * NK, True, False)
            with eng.Fori(g * NK + 1, (g + 1) * NK - 1) as i:
                step(i, False, False)
            step((g + 1) * NK - 1, False, True)

        def tiles_in(i, g):
            return 16 + (i // BT) * 16 * PIECES + g * 16 * (TT - PIECES)

        @block.gpsimd
        def _(pool):
            n = 0

            def const(ins):
                nonlocal n
                n += 1
                ins.then_inc(s_const, 1)
                pool.wait_ge(s_const, n)

            const(pool.memset(ident[:], 1.0))
            const(pool.affine_select(out=ident[:], in_=ident[:], compare_op=ALU.is_equal, fill=0.0,
                                     base=0, pattern=[[-1, P]], channel_multiplier=1))
            const(pool.memset(own[:], 1.0))
            const(pool.affine_select(out=own[:], in_=own[:], compare_op=ALU.is_ge, fill=0.0,
                                     base=0, pattern=[[-N, UC]], channel_multiplier=1))
            const(pool.affine_select(out=own[:], in_=own[:], compare_op=ALU.is_ge, fill=0.0,
                                     base=N - 1, pattern=[[N, UC]], channel_multiplier=-1))
            const(pool.iota(back[:], pattern=[[-1, P]], base=P - 1, channel_multiplier=0,
                            allow_small_or_imprecise_dtypes=True))
            const(pool.memset(last[:], 0.0))
            const(pool.memset(last[:, P - 1:P], 1.0))
            const(pool.memset(zero, 0.0))
            const(pool.memset(eps[:], EPS))
            const(pool.memset(wb[:], 0.0))
            cv = far[:, 0:UC * P].rearrange("p (j t) -> p j t", j=UC)
            const(pool.iota(cv, pattern=[[0, UC], [1, P]], base=1, channel_multiplier=0,
                            allow_small_or_imprecise_dtypes=True))
            const(pool.affine_select(out=cv, in_=cv, compare_op=ALU.is_ge, fill=FAR,
                                     base=0, pattern=[[-N, UC], [0, P]], channel_multiplier=1))
            const(pool.affine_select(out=cv, in_=cv, compare_op=ALU.is_ge, fill=FAR,
                                     base=N - 1, pattern=[[N, UC], [0, P]], channel_multiplier=-1))
            const(pool.memset(far[:, UC * P:], float(P)))
            const(pool.memset(far[:, UC * P:].rearrange("p (b c) -> p b c", b=HB)[:, :, 0:1], FAR))
            const(pool.memset(shift_s[:], 0.0))

            const(pool.iota(e_of, pattern=[[1, E], [0, TT]], base=0, channel_multiplier=0,
                            allow_small_or_imprecise_dtypes=True))
            const(pool.iota(tok8[:], pattern=[[E, TT]], base=0, channel_multiplier=E * TT,
                            allow_small_or_imprecise_dtypes=True))
            const(pool.memset(ones, 1.0))
            const(pool.memset(tri, 1.0))
            const(pool.affine_select(out=tri, in_=tri, compare_op=ALU.is_gt, fill=0.0,
                                     base=0, pattern=[[1, P]], channel_multiplier=-1))
            const(pool.iota(t_of, pattern=[[1, RT], [0, E]], base=0, channel_multiplier=0,
                            allow_small_or_imprecise_dtypes=True))
            const(pool.memset(slots_i[:], NOWHERE))
            const(pool.memset(pick_g[:], NOWHERE))
            const(pool.memset(pick_s[:], NOWHERE))
            const(pool.memset(stage_p[:], NOWHERE))
            const(pool.memset(stage_r[:], NOWHERE))
            const(pool.memset(t_e[:], 0))

            def keep(q):
                for k in range(LBUF):
                    at = q * (LBUF * LR) + k * LR
                    if not isinstance(at, int):
                        at = pool.snap(at)
                    if isinstance(q, int):
                        pool.wait_ge(s_load[k], 16 * (q + 1))
                    else:
                        hold(pool, s_load[k], 16 * (q + 1), s_const)
                    pool.tensor_copy(xb_row[:, bass.ds(at, LR), :], loadbuf[:, k, :, 0:P]).then_inc(s_keep, 1)

            keep(0)
            with pool.Fori(1, NL // LBUF) as q:
                keep(q)

            pool.wait_ge(s_rt, NROUTE)
            pool.wait_ge(s_slot0, 16)
            pool.wait_ge(s_dv, DV_STATS)
            pos_col = posi[:].rearrange("p k j -> p (k j)")
            row_col = rowi[:].rearrange("p k j -> p (k j)")

            def send(i, k):
                col = 2 * i + k
                if not isinstance(i, int):
                    col = pool.snap(col)
                wait(pool, s_scat[k], 16 * i)
                pool.tensor_copy(stage_p[:, k:k + 1], pos_col[:, bass.ds(col, 1)]).then_inc(s_stg, 1)
                pool.tensor_copy(stage_r[:, k:k + 1], row_col[:, bass.ds(col, 1)]).then_inc(s_stg, 1)
                hold(pool, s_stg, 2 * (2 * i + k + 1), s_const)
                pool.indirect_dma_start(
                    out=slot_d.rearrange("a b -> (a b)")[:, None],
                    out_offset=bass.IndirectOffsetOnAxis(ap=stage_p[:, k:k + 1], axis=0),
                    in_=stage_r[:, k:k + 1], in_offset=None,
                    bounds_check=RT * P - 1, oob_is_err=False).then_inc(s_scat[k], 16)

            def centres(g):
                def centre(i, first, final):
                    for k in range(2):
                        u = 2 * i + k
                        wait(pool, s_x, tiles_in(i, g))
                        wait(pool, s_xn, u - 1)
                        pool.tensor_tensor(cen[:, k].rearrange("p d r -> p r d"), unit_view(pool, i, k),
                                           mean[:, g * P:(g + 1) * P][:, :, None].to_broadcast([P, P, UC]),
                                           ALU.subtract).then_inc(s_cen, 1)
                        if g == 0:
                            send(i, k)
                over_blocks(pool, g, centre)

            centres(0)

            for k in range(2):
                pool.wait_ge(s_td[k], 16 * (TT // 2))
            pool.wait_ge(s_sf, 3)
            pool.wait_ge(s_zero, 16 * TT)
            pool.wait_ge(s_zf, 2)

            def gather(t, k):
                tt = t if isinstance(t, int) else pool.snap(t)
                wait(pool, s_g[k], 16 * (t // 2))
                wait(pool, s_gt, t - 1)
                pool.tensor_copy(pick_g[:, k:k + 1], slots[:, bass.ds(tt, 1)]).then_inc(s_pg, 1)
                hold(pool, s_pg, t + 1, s_const)
                pool.indirect_dma_start(
                    out=route_a[:, k, :], out_offset=None, in_=a_d.rearrange("t (e r) -> (t e) r", e=E),
                    in_offset=bass.IndirectOffsetOnAxis(ap=pick_g[:, k:k + 1], axis=0),
                    bounds_check=T * E - 1, oob_is_err=False).then_inc(s_g[k], 16)

            def scatter(t, k):
                tt = t if isinstance(t, int) else pool.snap(t)
                wait(pool, s_s[k], 16 * (t // 2))
                pool.tensor_copy(pick_s[:, k:k + 1], slots[:, bass.ds(tt, 1)]).then_inc(s_pk, 1)
                hold(pool, s_pk, t + 1, s_const)
                wait(pool, s_y, t + 1)
                pool.indirect_dma_start(
                    out=r_d.rearrange("t (e r) -> (t e) r", e=E),
                    out_offset=bass.IndirectOffsetOnAxis(ap=pick_s[:, k:k + 1], axis=0),
                    in_=route_y[:, k, :], in_offset=None,
                    bounds_check=T * E - 1, oob_is_err=False).then_inc(s_s[k], 16)

            gather(0, 0)
            gather(1, 1)
            gather(2, 0)
            gather(3, 1)
            scatter(0, 0)
            gather(4, 0)
            scatter(1, 1)
            gather(5, 1)
            scatter(2, 0)
            with pool.Fori(3, RT // 2) as q:
                gather(q * 2, 0)
                scatter(q * 2 - 3, 1)
                gather(q * 2 + 1, 1)
                scatter(q * 2 - 2, 0)
            scatter(RT - 3, 1)
            scatter(RT - 2, 0)
            scatter(RT - 1, 1)

            pool.wait_ge(s_dv, 2 * DV_STATS)
            centres(1)

        @block.sync
        def _(sp):
            def piece(g, t, j, per=PR):
                v = (t % 2) * P + j * per, g * P + j * per, (t % DG) * P
                return [a if isinstance(a, int) else sp.snap(a) for a in v]

            def load_tile(g, t, pieces, after=None, value=0, per=PR):
                for j in pieces:
                    r0, row, d0 = piece(g, t, j, per)
                    if after is not None:
                        wait(sp, after, value + 16 * (j + 1))
                    sp.dma_start(xb_row[:, bass.ds(r0, per), :], x_rows[:, bass.ds(row, per), bass.ds(d0, P)])\
                      .then_inc(s_x, 16)

            def store_tile(g, t, pieces):
                for j in pieces:
                    r0, _, d0 = piece(g, t, j)
                    sp.dma_start(o_rows[g * P:(g + 1) * P, j * PR:(j + 1) * PR, bass.ds(d0, P)],
                                 xb_row[:, bass.ds(r0, PR), :]).then_inc(s_out, 16)

            def store_rows(g, t, a, z, pieces, done):
                n, r0, d0 = P // pieces, (t % 2) * P, (t % DG) * P
                return [lambda j=j: sp.dma_start(
                    o_rows[g * P + a:g * P + z, j * n:(j + 1) * n, d0:d0 + P],
                    xb_row[a:z, r0 + j * n:r0 + (j + 1) * n, :]).then_inc(done, 16) for j in range(pieces)]

            for j, a in enumerate((delta, alpha, beta)):
                sp.dma_start(par[:, j, :], a.rearrange("(u d) n o -> u (d n o)", d=UC)).then_inc(s_par, 16)
            sp.dma_start(par[:, 3, :], gamma.rearrange("(u d) n -> u (d n)", d=UC)).then_inc(s_par, 16)
            sp.dma_start(om[:], omega.rearrange("(a d) -> a d", a=1)).then_inc(s_om, 16)
            sp.dma_start(idx[:], ei.rearrange("(p j) k -> p j k", p=P)).then_inc(s_idx, 16)
            sp.dma_start(wgt[:], ew.rearrange("(p j) k -> p j k", p=P)).then_inc(s_idx, 16)
            for k in range(LBUF):
                sp.dma_start(loadbuf[:, k], x_rows[:, k * LR:(k + 1) * LR, :]).then_inc(s_load[k], 16)
            with sp.Fori(1, NL // LBUF) as q:
                for k in range(LBUF):
                    at = sp.snap(q * (LBUF * LR) + k * LR)
                    read = (q - 1) * LBUF + k + 1
                    now(sp, read)
                    wait(sp, s_free, read)
                    wait(sp, s_keep, read)
                    sp.dma_start(loadbuf[:, k], x_rows[:, bass.ds(at, LR), :])\
                        .then_inc(s_load[k], 16)
            sp.wait_ge(s_const, NCONST)
            sp.dma_start(slot_d, slots_i[:]).then_inc(s_slot0, 16)
            sp.wait_ge(s_cp, NK)
            sp.dma_start(taps_d[:, P:P + ZR, :].rearrange("k i d -> i k d"), zero[0:ZR]).then_inc(s_tab, 16)
            sp.wait_ge(s_tab, 16)
            sp.wait_ge(s_keep, NL)
            sp.dma_start(taps_d[:, 0:P, :].rearrange("k i d -> i k d"), taps).then_inc(s_x, 16)
            sp.wait_ge(s_x, 16)
            sp.wait_ge(s_dec, 16 * NK)

            def load_weights(i):
                kb, h = i % NK, i % 2
                if not isinstance(i, int):
                    kb, h = sp.snap(kb), sp.snap(h)
                dst = wb[:, bass.ds(h, 1)].rearrange("p h m d -> p (h m) d")
                row = taps_d[bass.ds(kb, 1)].rearrange("k i d -> k (i d)")
                dec = decay_d[bass.ds(kb, 1)].rearrange("k s n d -> (k s) n d")
                loads, read = 16 * WL * i, 2 * (i - 1)
                now(sp, loads, read)
                wait(sp, s_w, loads)
                wait(sp, s_loc, read)
                for s0 in range(0, P, P // 4):
                    reach = P - s0
                    src = bass.AP(row.tensor, row.offset + s0 * KD, [[KD, P // 4], [1, reach * KD]])
                    sp.dma_start(dst[s0:s0 + P // 4, N:N + reach, :], src).then_inc(s_w, 16)
                sp.dma_start(dst[:, 0:N, :], dec).then_inc(s_w, 16)

            weights = [(load1a, w1a.rearrange("(m p) d -> p m d", p=P))]
            weights += [(load2a[:, m, :], w2a[m * P:(m + 1) * P, :]) for m in range(KC)]

            def tile(g, t, first, final):
                for b in range(BT):
                    if not (first and g == 1 and b < 2):
                        load_weights(t * BT + b)
                    if b == 1 and not first:
                        wait(sp, s_ev, 3 * UT * t)
                    for j in range(2 * PIECES * (b - 1) // (BT - 1), 2 * PIECES * b // (BT - 1)):
                        if first and 0 <= j < PIECES:
                            load_tile(g, t + 1, [j])
                        elif not first and 0 <= j < PIECES:
                            store_tile(g, t - 1, [j])
                        elif PIECES <= j < 2 * PIECES and not first and not final:
                            load_tile(g, t + 1, [j - PIECES], s_out, 16 * PIECES * (t - 1))
                    if final and g == 0 and 4 <= b < 4 + len(weights):
                        if b == 4:
                            sp.wait_ge(s_out, 16 * PIECES * t)
                        for dst, src in weights[2 * (b - 4):2 * (b - 3)]:
                            sp.dma_start(dst, src).then_inc(s_wl, 16)

            def tiles(g):
                t0 = g * DG
                tile(g, t0, True, False)
                with sp.Fori(t0 + 1, t0 + DG - 1) as t:
                    tile(g, t, False, False)
                tile(g, t0 + DG - 1, False, True)

            tiles(0)
            sp.wait_ge(s_ev, 3 * UT * DG)
            for store in store_rows(0, DG - 1, 0, CH, 2, s_first):
                store()
            others = store_rows(0, DG - 1, CH, P, PIECES, s_out)
            sp.wait_ge(s_first, 32)

            for k in range(2):
                sp.wait_ge(s_scat[k], 16 * NK)
            sp.dma_start(slots_i[:], slot_d).then_inc(s_slots, 16)

            x_tok = out.rearrange("b l d -> (b l) d")[0:T].rearrange("(p j) d -> j p d", j=TT)
            a_tok = a_d.rearrange("(p j) r -> j p r", j=TT)
            r_tok = r_d.rearrange("(p j) r -> j p r", j=TT)

            def one(ap, j):
                if not isinstance(j, int):
                    j = sp.snap(j)
                return ap[bass.ds(j, 1)].rearrange("a p d -> (a p) d")

            def tok_load(j, k):
                wait(sp, s_tn, j - 1)
                sp.dma_start(tok_x[:, k, :], one(x_tok, j)).then_inc(s_tx[k], 16)

            def tok_store(j, k):
                v = one(a_tok, j)
                wait(sp, s_tb, j + 1)
                sp.dma_start(v, tok_a[:, k, :]).then_inc(s_td[k], 16)
                sp.dma_start(one(r_tok, j), zeros_f).then_inc(s_zero, 16)

            def tok_load_first(j, k):
                tok_load(j, k)
                if isinstance(j, int) and j < 4:
                    for store in others[PIECES // 4 * j:PIECES // 4 * (j + 1)]:
                        store()
                if isinstance(j, int) and j == 2:
                    sp.wait_ge(s_zf, 1)

            in_pairs(sp, TT, tok_load_first, tok_store, lag=3)
            sp.wait_ge(s_out, 16 * PIECES * DG)

            def up_load(t, k):
                tt = t if isinstance(t, int) else sp.snap(t)
                e = sp.value_load(t_e[0:1, bass.ds(tt, 1)], min_val=0, max_val=E - 1)
                row = sp.snap(e * RANK)
                wait(sp, s_up, 4 * (t - 1))
                sp.dma_start(w1bs[:, k, :], w1b[bass.ds(row, RANK), :]).then_inc(s_wu[k], 16)

            def up_loads(q, first_tile):
                for k in range(2):
                    up_load(q * 2 + k, k)
                if isinstance(q, int) and q == 0:
                    sp.wait_ge(s_wt, KC + FC)
                if first_tile:
                    load_tile(1, DG, [q * 2, q * 2 + 1], per=P // TT)

            up_loads(0, True)
            up_loads(1, True)
            with sp.Fori(2, TT // 2) as q:
                up_loads(q, True)
            with sp.Fori(TT // 2, RT // 2) as q:
                up_loads(q, False)

            load_weights(NK)
            load_weights(NK + 1)
            sp.wait_ge(s_dv, 2 * DV_STATS)
            sp.wait_ge(s_dn, RT)
            tiles(1)

            for k in range(2):
                sp.wait_ge(s_s[k], 16 * (RT // 2))
            sp.wait_ge(s_out, 16 * PIECES * (NT - 1))
            sp.dma_start(w2bs, w2b.rearrange("(k p) d -> p k d", p=P)).then_inc(s_wl, 16)
            for k in range(2):
                sp.dma_start(res_x[:, k, :], one(x_tok, k)).then_inc(s_rx[k], 16)

            def res_load(j, k):
                v = one(r_tok, j)
                wait(sp, s_rw, j - 1)
                sp.dma_start(res_a[:, k, :], v).then_inc(s_rr[k], 16)

            def res_store(j, k):
                v = one(x_tok, j)
                wait(sp, s_r4, j + 1)
                sp.dma_start(v, res_o[:, k, :]).then_inc(s_r5[k], 16)
                if not (isinstance(j, int) and j >= TT - 2):
                    sp.dma_start(res_x[:, k, :], one(x_tok, j + 2)).then_inc(s_rx[k], 16)
                if isinstance(j, int) and j == 0:
                    sp.wait_ge(s_ev, 3 * UT * NT)
                n = P // TT
                at = j * n if isinstance(j, int) else sp.snap(j * n)
                row = P + at if isinstance(j, int) else sp.snap(P + j * n)
                sp.dma_start(o_rows[P:2 * P, bass.ds(at, n), (DG - 1) * P:],
                             xb_row[:, bass.ds(row, n), :]).then_inc(s_out, 16)

            in_pairs(sp, TT, res_load, res_store, lag=3)
            for k in range(2):
                sp.wait_ge(s_r5[k], 16 * (TT // 2))
            sp.wait_ge(s_out, 16 * PIECES * (NT - 1) + 16 * TT)

        @block.scalar
        def _(act):
            act.wait_ge(s_par, 64)
            act.activation(par[:, 4, :], par[:, 0, :], ACT.Sigmoid).then_inc(s_prep, 1)
            act.activation(par[:, 5, :], par[:, 1, :], ACT.Sigmoid).then_inc(s_prep, 1)
            act.wait_ge(s_prep, 4)
            act.activation(par[:, 7, :], par[:, 6, :], ACT.Ln).then_inc(s_prep, 1)
            act.wait_ge(s_prep, 11)

            def table(i, h):
                wait(act, s_tap, i - 1)
                for k in range(2):
                    col = 2 * i + k
                    col = col if isinstance(col, int) else act.snap(col)
                    act.activation(decay[:, 2 * h + k, :], back[:], ACT.Exp, scale=rate[:, bass.ds(col, 1)])\
                       .then_inc(s_exp, 1)

            def decays_out(i):
                ii = i if isinstance(i, int) else act.snap(i)
                dst = decay_d[bass.ds(ii, 1)].rearrange("k s n d -> s k (n d)")
                src = decays[:, bass.ds(ii, 1)].rearrange("p k n d -> p k (n d)")
                wait(act, s_cp, i + 1)
                act.dma_start(dst, src).then_inc(s_dec, 16)

            def table_out(i, h):
                if not (isinstance(i, int) and i == 0):
                    decays_out(i - 1)
                ii = i if isinstance(i, int) else act.snap(i)
                wait(act, s_tap, i + 1)
                act.activation(taps[:, bass.ds(ii, 1), :].rearrange("p k d -> p (k d)"), ps[:, 4 * h, 0:KD],
                               ACT.Copy)
                for k in range(2):
                    dst = decays[:, bass.ds(ii, 1), :, k * UC:(k + 1) * UC].rearrange("p k n d -> p (k n) d")
                    ins = act.activation(dst.rearrange("p n d -> p d n"),
                                         ps[:, 4 * h + 1, k * P:(k + 1) * P]
                                         .rearrange("p (d n) -> p d n", d=UC)[:, :, ::-1], ACT.Copy)
                ins.then_inc(s_cp, 1)

            act.wait_ge(s_const, NCONST)
            in_pairs(act, NK, table, table_out, lag=1)

            def deviations(g):
                act.wait_ge(s_dv, (g + 1) * DV_STATS - 1)
                act.activation(rstd[:, g * P:(g + 1) * P], var[:, g * P:(g + 1) * P], ACT.Sqrt,
                               bias=eps[:, 0:1]).then_inc(s_std, 1)

            decays_out(NK - 1)
            deviations(0)

            def evacuate(i, k):
                u = 2 * i + k
                view = unit_view(act, i, k)
                for b, (a, z) in enumerate(BANKS):
                    wait(act, s_pe, 3 * u + b + 1)
                    act.activation(view[:, :, a:z].rearrange("p t d -> p d t"),
                                   ps[:, 3 * k + b, 0:NI * (z - a)].rearrange("p (d t) -> p d t", t=NI)[:, :, 0:P],
                                   ACT.Copy).then_inc(s_ev, 1)

            def steps(i, first, final):
                for k in range(2):
                    u = 2 * i + k
                    col = 2 * (i % NK) + k
                    if not isinstance(i, int):
                        col = act.snap(col)
                    wait(act, s_pe, 3 * (u - 1))
                    act.activation(carry[:, k, :], far[:], ACT.Exp, scale=rate[:, bass.ds(col, 1)])\
                       .then_inc(s_ca, 1)
                    if not (first and k == 0):
                        evacuate(i if k == 1 else i - 1, 1 - k)
                    wait(act, s_tr, u + 2)
                    wait(act, s_st, u - 1)
                    act.activation(shift_s[:, k, :, 1:CH],
                                   ps[:, 6 + k, 0:P].rearrange("p (b c) -> p b c", b=HB)[:, :, 0:CH - 1],
                                   ACT.Copy, scale=coef[:, bass.ds(col, 1)]).then_inc(s_sh, 1)

            act.wait_ge(s_rt, NROUTE)
            over_blocks(act, 0, steps)
            evacuate(NK - 1, 1)

            def weights_out(c0, c1):
                for c in range(c0, c1):
                    dst = w1at[:, c, :] if c < KC else w2at[:, c - KC, 0:ER]
                    act.wait_ge(s_wt, c + 1)
                    act.activation(dst, ps[:, c % 2, :], ACT.Copy).then_inc(s_wc, 1)

            weights_out(0, KC)

            def deviation(j, k):
                wait(act, s_tv, j + 1)
                act.activation(tstat[:, k, 8:9], tstat[:, k, 7:8], ACT.Sqrt, bias=eps[:, 0:1]).then_inc(s_ts, 1)

            def turned(j, k):
                wait(act, s_tt, j + 1)
                act.activation(tok_t[:, k, :], ps[:, k, :], ACT.Copy).then_inc(s_tc, 1)

            in_pairs(act, TT, deviation, turned, lag=1)

            def gelus(t, k):
                for b in range(4):
                    wait(act, s_up, 4 * t + b + 1)
                    if b == 0:
                        wait(act, s_dn, t - 1)
                    n4 = FC // 4
                    act.activation(act_h[k][:, b * n4:(b + 1) * n4, :].rearrange("p f r -> p (f r)"),
                                   ps[:, b, :], ACT.Gelu).then_inc(s_ge, 1)

            act.wait_ge(s_out, 16 * PIECES * DG)
            weights_out(KC, KC + FC)
            def load2(n, k):
                at = P + n * LR2
                if not isinstance(n, int):
                    at = act.snap(at)
                wait(act, s_free2, n - 1)
                act.dma_start(ring2[:, k], x_rows[:, bass.ds(at, LR2), :]).then_inc(s_load2[k], 16)

            def gelu_pair(q, load):
                for k in range(2):
                    gelus(q * 2 + k, k)
                    if load:
                        load2(q * 2 - 2 + k, k)

            gelu_pair(0, False)
            gelu_pair(1, True)
            with act.Fori(2, NL2 // 2 + 1) as q:
                gelu_pair(q, True)
            for q in range(NL2 // 2 + 1, QS):
                gelu_pair(q, False)
            deviations(1)
            with act.Fori(QS, RT // 2) as q:
                gelu_pair(q, False)

            over_blocks(act, 1, steps)
            evacuate(NB - 1, 1)

            def results(j, k):
                wait(act, s_r1, j + 1)
                act.activation(res_t[:, k, :], ps[:, 6 + k, :], ACT.Copy).then_inc(s_r2, 1)

            in_pairs(act, TT, results)

        @block.vector
        def _(dve):
            stats1 = raw_row[:, 0:6 * P].rearrange("p (r f) -> p r f", f=6)

            def row_stats(q):
                for k in range(LBUF):
                    wait(dve, s_load[k], 16 * (q + 1))
                    for r in range(LR):
                        at = q * (LBUF * LR) + k * LR + r
                        if not isinstance(q, int):
                            at = dve.snap(at)
                        ins = dve.bn_stats(stats1[:, bass.ds(at, 1), :].rearrange("p a b -> p (a b)"),
                                           loadbuf[:, k, r, :])
                    ins.then_inc(s_free, 1)

            def row_stats_rest():
                with dve.Fori(3, NL // LBUF) as q:
                    row_stats(q)
                dve.wait_ge(s_free, NL)

            def row_stats2(n, k):
                wait(dve, s_load2[k], 16 * (n // 2 + 1))
                for r in range(LR2):
                    at = n * LR2 + r
                    if not isinstance(n, int):
                        at = dve.snap(at)
                    ins = dve.bn_stats(stats2[:, bass.ds(at, 1), :].rearrange("p a b -> p (a b)"),
                                       ring2[:, k, r, :])
                ins.then_inc(s_free2, 1)

            def statistics(g, st_of):
                n = g * DV_STATS

                def chain(ins):
                    nonlocal n
                    n += 1
                    ins.then_inc(s_dv, 1)
                    dve.wait_ge(s_dv, n)

                st = st_of.rearrange("p r f -> p f r")
                m, v, r = (a[:, g * P:(g + 1) * P] for a in (mean, var, rstd))
                chain(dve.tensor_tensor(m, st[:, 1, :], st[:, 4, :], ALU.add))
                chain(dve.tensor_scalar(m, m, 0.5, None, ALU.mult))
                chain(dve.tensor_tensor(r, st[:, 1, :], st[:, 4, :], ALU.subtract))
                chain(dve.tensor_tensor(r, r, r, ALU.mult))
                chain(dve.tensor_scalar(r, r, D / 4.0, None, ALU.mult))
                chain(dve.tensor_tensor(r, r, st[:, 2, :], ALU.add))
                chain(dve.tensor_tensor(r, r, st[:, 5, :], ALU.add))
                chain(dve.tensor_scalar(v, r, 1.0 / D, None, ALU.mult))
                dve.wait_ge(s_std, g + 1)
                chain(dve.reciprocal(r, r))
                assert n == (g + 1) * DV_STATS

            dve.wait_ge(s_prep, 2)
            dve.tensor_tensor(par[:, 6, :], par[:, 4, :], par[:, 5, :], ALU.mult).then_inc(s_prep, 1)
            dve.wait_ge(s_prep, 3)
            dve.tensor_scalar(par[:, 6, :], par[:, 6, :], -1.0, 1.0, ALU.mult, ALU.add).then_inc(s_prep, 1)
            dve.wait_ge(s_prep, 5)
            dve.tensor_scalar(par[:, 7, :], par[:, 7, :], -TINY, None, ALU.min).then_inc(s_prep, 1)
            dve.tensor_tensor(par[:, 4, :], par[:, 4, :], par[:, 2, :], ALU.mult).then_inc(s_prep, 1)
            dve.wait_ge(s_prep, 7)
            dve.tensor_scalar(par[:, 3, :], par[:, 3, :], (1.0 / N) ** 0.5, None, ALU.mult).then_inc(s_prep, 1)
            dve.wait_ge(s_prep, 8)
            dve.tensor_tensor(par[:, 4, :], par[:, 4, :], par[:, 3, :], ALU.mult).then_inc(s_prep, 1)
            row_stats(0)
            dve.wait_ge(s_tr, 1)
            dve.tensor_copy(rate[:], ps[:, 2, 0:NU]).then_inc(s_prep, 1)
            dve.tensor_copy(coef[:], ps[:, 2, NU:2 * NU]).then_inc(s_prep, 1)
            dve.wait_ge(s_prep, 11)
            dve.wait_ge(s_const, NCONST)
            dve.tensor_tensor(coef8, coef[:][:, :, None].to_broadcast([P, NU, UC]),
                              own[:][:, None, :].to_broadcast([P, NU, UC]), ALU.mult).then_inc(s_prep, 1)

            def routing():
                n = 0

                def rt(ins):
                    nonlocal n
                    n += 1
                    ins.then_inc(s_rt, 1)
                    dve.wait_ge(s_rt, n)

                def over_e(ap):
                    return ap[:, :, None].to_broadcast([P, E, TT])

                def over_t(ap):
                    return ap[:, None, :].to_broadcast([P, E, TT])

                dve.wait_ge(s_idx, 32)
                rt(dve.tensor_copy(idf[:], idx[:]))
                for k in range(TK):
                    rt(dve.tensor_tensor(hot[:, k], over_t(idf[:, :, k]), e_of, ALU.is_equal))
                rt(dve.tensor_tensor(hot[:, 2], hot[:, 0], hot[:, 1], ALU.max))
                rt(dve.tensor_tensor(route_w[:], hot[:, 0], over_t(wgt[:, :, 0]), ALU.mult))
                rt(dve.tensor_tensor(tmp_e, hot[:, 1], over_t(wgt[:, :, 1]), ALU.mult))
                rt(dve.tensor_tensor(route_w[:], route_w[:], tmp_e, ALU.add))
                for e in range(E):
                    rt(dve.tensor_tensor_scan(rank_in[:, e, :], ones[:, 0:TT], hot[:, 2, e, :], 0.0,
                                              ALU.mult, ALU.add))
                rt(dve.tensor_copy(small[:, 0, :], rank_in[:, :, TT - 1]))
                yield
                dve.wait_ge(s_rp, 1)
                rt(dve.tensor_copy(small[:, 1, :], ps[:, 3, 0:E]))
                rt(dve.tensor_scalar(smalli[:], ps[:, 3, E:2 * E], float(P - 1), None, ALU.add))
                rt(dve.tensor_scalar(smalli[:], smalli[:], P.bit_length() - 1, None, ALU.arith_shift_right))
                rt(dve.tensor_copy(small[:, 2, :], smalli[:]))
                rt(dve.tensor_tensor_scan(small[:, 3, :], ones[:, 0:E], small[:, 2, :], 0.0, ALU.mult, ALU.add))
                rt(dve.tensor_tensor(small[:, 4, :], small[:, 3, :], small[:, 2, :], ALU.subtract))
                rt(dve.tensor_scalar(small[:, 4, :], small[:, 4, :], float(P), -1.0, ALU.mult, ALU.add))
                rt(dve.tensor_tensor(small[:, 4, :], small[:, 4, :], small[:, 1, :], ALU.add))
                rt(dve.tensor_tensor(rank_in, rank_in, over_e(small[:, 4, :]), ALU.add))
                yield
                for k in range(TK):
                    rt(dve.tensor_reduce(flag[:], hot[:, k].rearrange("p e j -> p j e"), AX_X, ALU.add))
                    rt(dve.tensor_scalar(flag[:], flag[:], -float(NOWHERE), float(NOWHERE), ALU.mult, ALU.add))
                    rt(dve.tensor_tensor(tmp_e, hot[:, k], rank_in, ALU.mult))
                    rt(dve.tensor_reduce(posf[:, k, :], tmp_e.rearrange("p e j -> p j e"), AX_X, ALU.add))
                    rt(dve.tensor_tensor(posf[:, k, :], posf[:, k, :], flag[:], ALU.add))
                    rt(dve.tensor_tensor(rowf[:, k, :], idf[:, :, k], tok8[:], ALU.add))
                rt(dve.tensor_tensor(tmp_e, hot[:, 0], hot[:, 1], ALU.mult))
                rt(dve.tensor_reduce(flag[:], tmp_e.rearrange("p e j -> p j e"), AX_X, ALU.add))
                rt(dve.tensor_scalar(flag[:], flag[:], float(NOWHERE), None, ALU.mult))
                rt(dve.tensor_tensor(posf[:, 1, :], posf[:, 1, :], flag[:], ALU.add))
                rt(dve.tensor_copy(posi[:], posf[:]))
                rt(dve.tensor_copy(rowi[:], rowf[:]))
                rt(dve.tensor_tensor(t_le, small[0:1, 3, :][:, None, :].to_broadcast([1, RT, E]), t_of,
                                     ALU.is_le))
                rt(dve.tensor_reduce(t_ef[:], t_le, AX_X, ALU.add))
                rt(dve.tensor_scalar(t_ef[:], t_ef[:], float(E - 1), None, ALU.min))
                rt(dve.tensor_copy(t_e[:], t_ef[:]))
                assert n == NROUTE, n
                yield

            parts = routing()
            next(parts)
            row_stats(1)
            next(parts)
            row_stats(2)
            next(parts)
            row_stats_rest()
            statistics(0, stats1)

            def stage(g, i, k):
                u = 2 * i + k
                wait(dve, s_x, tiles_in(i, g))
                wait(dve, s_loc, u - 1)
                dve.tensor_copy(raw[:, k].rearrange("p d r -> p r d"), unit_view(dve, i, k)).then_inc(s_raw, 1)
                wait(dve, s_cen, u + 1)
                dve.tensor_tensor(xn[:, k], cen[:, k],
                                  rstd[:, g * P:(g + 1) * P][:, None, :].to_broadcast([P, UC, P]),
                                  ALU.mult).then_inc(s_xn, 1)

            def steps(g, i, first, final):
                for k in range(2):
                    u = 2 * i + k
                    if not (final and k == 1):
                        stage(g, i if k == 0 else i + 1, 1 - k)
                    wait(dve, s_loc, u + 1)
                    wait(dve, s_tr, u)
                    dst = chunk_s[:, k, :].rearrange("p (d n) -> p d n", n=N)
                    src = ps[:, 3 * k:3 * k + 2, 0:3 * NI].rearrange("p a (d m) -> p a d m", m=NI)[:, :, :, P:]
                    dve.tensor_copy(dst[:, 0:6].rearrange("p (a d) n -> p a d n", a=2), src).then_inc(s_cs, 1)
                    src = ps[:, 3 * k + 2, 0:2 * NI].rearrange("p (d m) -> p d m", m=NI)[:, :, P:]
                    dve.tensor_copy(dst[:, 6:8], src).then_inc(s_cs, 1)
                    wait(dve, s_sh, u + 1)
                    wait(dve, s_ca, u + 1)
                    wait(dve, s_pe, 3 * (u - 1))
                    dve.tensor_tensor_scan(state[:, k, :], carry[:, k, UC * P:],
                                           shift_s[:, k].rearrange("p b c -> p (b c)"), 0.0,
                                           ALU.mult, ALU.add).then_inc(s_st, 1)

            stage(0, 0, 0)
            over_blocks(dve, 0, lambda i, first, final: steps(0, i, first, final))
            dve.wait_ge(s_pe, 3 * UT * DG)
            dve.memset(zeros_f, 0.0).then_inc(s_zf, 1)
            dve.memset(route_a, 0.0).then_inc(s_zf, 1)
            dve.wait_ge(s_slots, 16)
            dve.tensor_copy(slots_f, slots_i[:]).then_inc(s_sf, 1)
            dve.wait_ge(s_sf, 2)
            dve.tensor_copy(slots[:], ps[:, 4, 0:RT]).then_inc(s_sf, 1)

            def tokens(j, k):
                st, m = tstat[:, k, 0:6], tstat[:, k, 6:8]
                wait(dve, s_tx[k], 16 * (j // 2 + 1))
                dve.bn_stats(st, tok_x[:, k, :]).then_inc(s_ch, 1)
                hold(dve, s_ch, 2 * j + 1, s_const)
                dve.bn_aggr(m, st).then_inc(s_tv, 1)
                wait(dve, s_ts, j + 1)
                dve.reciprocal(tstat[:, k, 9:10], tstat[:, k, 8:9]).then_inc(s_ch, 1)
                wait(dve, s_ch, 2 * j + 2)
                wait(dve, s_tt, j - 1)
                dve.tensor_scalar(tok_n[:, k, :], tok_x[:, k, :], tstat[:, k, 6:7], tstat[:, k, 9:10],
                                  ALU.subtract, ALU.mult).then_inc(s_tn, 1)

            def ranks(j, k):
                wait(dve, s_ta, j + 1)
                wait(dve, s_td[k], 16 * (j // 2))
                dve.tensor_copy(tok_a[:, k, :], ps[:, 2 + k, :]).then_inc(s_tb, 1)

            in_pairs(dve, TT, tokens, ranks)
            dve.wait_ge(s_out, 16 * PIECES * DG)
            dve.memset(w2at[:, :, ER:], 0.0).then_inc(s_zf, 1)

            def routes_in(t, k):
                wait(dve, s_gt, t + 1)
                wait(dve, s_up, 4 * (t - 1))
                dve.tensor_copy(route_t[0:RANK, k, :], ps[0:RANK, 6 + k, 0:P]).then_inc(s_gc, 1)

            def routes_out(t, k):
                wait(dve, s_dn, t + 1)
                wait(dve, s_s[k], 16 * (t // 2))
                dve.tensor_copy(route_y[:, k, :], ps[:, 4 + k, 0:RANK]).then_inc(s_y, 1)

            routes_in(0, 0)
            routes_in(1, 1)
            routes_in(2, 0)
            routes_out(0, 0)
            routes_in(3, 1)
            routes_out(1, 1)
            for q0, q1 in ((2, QS), (QS, RT // 2)):
                with dve.Fori(q0, q1) as q:
                    for k in range(2):
                        routes_in(q * 2 + k, k)
                        routes_out(q * 2 - 2 + k, k)
                        if q1 == QS:
                            row_stats2(q * 2 - 4 + k, k)
                if q1 == QS:
                    dve.wait_ge(s_free2, NL2)
                    statistics(1, stats2)
            routes_out(RT - 2, 0)
            routes_out(RT - 1, 1)

            stage(1, NK, 0)
            for k in range(2):
                dve.wait_ge(s_s[k], 16 * (RT // 2))
            over_blocks(dve, 1, lambda i, first, final: steps(1, i, first, final))

            def weigh(j, k):
                jj = j if isinstance(j, int) else dve.snap(j)
                wait(dve, s_rr[k], 16 * (j // 2 + 1))
                wait(dve, s_r1, j - 1)
                dve.tensor_tensor(res_n[:, k, :].rearrange("p (e r) -> p e r", e=E),
                                  res_a[:, k, :].rearrange("p (e r) -> p e r", e=E),
                                  route_w[:, :, bass.ds(jj, 1)].to_broadcast([P, E, RANK]),
                                  ALU.mult).then_inc(s_rw, 1)

            def finish(j, k):
                wait(dve, s_rx[k], 16 * (j // 2 + 1))
                wait(dve, s_r3, j + 1)
                wait(dve, s_r5[k], 16 * (j // 2))
                dve.tensor_tensor(res_o[:, k, :], res_x[:, k, :], ps[:, 2 + k, :], ALU.add).then_inc(s_r4, 1)

            in_pairs(dve, TT, weigh, finish)

        @block.tensor
        def _(pe):
            pe.wait_ge(s_prep, 9)
            pe.wait_ge(s_const, NCONST)
            pe.transpose(ps[:, 2, 0:NU], par[:, 7, :], ident[0:NU, 0:NU])
            pe.transpose(ps[:, 2, NU:2 * NU], par[:, 4, :], ident[0:NU, 0:NU]).then_inc(s_tr, 1)
            pe.wait_ge(s_rt, 16)
            pe.matmul(ps[:, 3, 0:E], tri, small[:, 0, :], start=True, stop=True)
            pe.matmul(ps[:, 3, E:2 * E], ones, small[:, 0, :], start=True, stop=True).then_inc(s_rp, 1)
            pe.wait_ge(s_prep, 12)
            pe.wait_ge(s_om, 16)

            def table(i, h):
                wait(pe, s_cp, i - 1)
                for k in range(2):
                    u = 2 * i + k
                    wait(pe, s_exp, u + 1)
                    col = u if isinstance(u, int) else pe.snap(u)
                    o0 = u * UC if isinstance(u, int) else pe.snap(u * UC)
                    o = ps[:, 4 * h, k * UC:(k + 1) * UC]
                    pe.matmul(o, decay[:, 2 * h + k, :],
                              coef8[:, bass.ds(col, 1), :].rearrange("p a b -> p (a b)"),
                              start=True, stop=False, skip_group_check=True)
                    pe.matmul(o, last[:], om[:, bass.ds(o0, UC)],
                              start=False, stop=True, skip_group_check=True)
                    ins = pe.transpose(ps[:, 4 * h + 1, k * P:(k + 1) * P], decay[:, 2 * h + k, :], ident[:])
                ins.then_inc(s_tap, 1)

            in_pairs(pe, NK, table)
            pe.wait_ge(s_cp, NK)

            def local(i, k):
                u = 2 * i + k
                wait(pe, s_xn, u + 1)
                wait(pe, s_raw, u + 1)
                if k == 0:
                    wait(pe, s_w, 16 * WL * (i + 1))
                h = i % 2
                if not isinstance(i, int):
                    h = pe.snap(h)
                w = wb[:, bass.ds(h, 1)].rearrange("p h m d -> p (h m) d")
                for b, (a, z) in enumerate(BANKS):
                    wait(pe, s_ev, 3 * (u - 2) + b + 1)
                    for d in range(a, z):
                        o = ps[:, 3 * k + b, NI * (d - a):NI * (d - a + 1)]
                        pe.matmul(o[:, 0:P], raw[:, k, d, :], ident[:], start=(d == a), stop=False,
                                  is_transpose=True, skip_group_check=True)
                    for d in range(a, z):
                        o = ps[:, 3 * k + b, NI * (d - a):NI * (d - a + 1)]
                        c = k * UC + d
                        ins = pe.matmul(o[:, ::-1], xn[:, k, d, :], w[:, :, c:c + 1].rearrange("p m d -> p (m d)"),
                                        start=False, stop=(d == z - 1), skip_group_check=True)
                ins.then_inc(s_loc, 1)

            def between(i, k):
                u = 2 * i + k
                wait(pe, s_st, u + 1)
                for b, (a, z) in enumerate(BANKS):
                    o = ps[:, 3 * k + b, 0:NI * (z - a)].rearrange("p (d m) -> p d m", m=NI)[:, :, 0:P]
                    pe.matmul(o, state[:, k, :], carry[:, k, a * P:z * P].rearrange("p (d t) -> p d t", t=P),
                              start=False, stop=True, skip_group_check=True).then_inc(s_pe, 1)

            def steps(i, first, final):
                for k in range(2):
                    u = 2 * i + k
                    local(i, k)
                    if not (first and k == 0):
                        between(i if k == 1 else i - 1, 1 - k)
                    wait(pe, s_cs, 2 * (u + 1))
                    pe.transpose(ps[:, 6 + k, 0:P], chunk_s[:, k, :], ident[:]).then_inc(s_tr, 1)

            over_blocks(pe, 0, steps)
            between(NK - 1, 1)

            pe.wait_ge(s_ev, 3 * UT * DG)
            pe.wait_ge(s_wl, 16 * (1 + KC))

            def turn_weights(c0, c1):
                for c in range(c0, c1):
                    wait(pe, s_wc, c - 1)
                    for m in range(KC):
                        src = load1a[:, m, c * P:(c + 1) * P] if c < KC \
                            else load2a[:, m, (c - KC) * P:(c - KC + 1) * P]
                        ins = pe.transpose(ps[:, c % 2, m * P:(m + 1) * P], src, ident[:])
                    ins.then_inc(s_wt, 1)

            turn_weights(0, KC)
            pe.wait_ge(s_sf, 1)
            pe.transpose(ps[:, 4, 0:RT], slots_f, ident[0:RT, 0:RT]).then_inc(s_sf, 1)
            pe.wait_ge(s_wc, KC)

            def turn(j, k, src, bank, s_in, s_done):
                wait(pe, s_in, j + 1)
                for c in range(KC):
                    ins = pe.transpose(ps[:, bank + k, c * P:(c + 1) * P], src[:, k, c * P:(c + 1) * P], ident[:])
                ins.then_inc(s_done, 1)

            def product(j, k, turned, w, s_in, s_freed, s_done):
                wait(pe, s_in, j + 1)
                wait(pe, s_freed, j - 1)
                if isinstance(j, int) and j == 0 and w is w2bs:
                    pe.wait_ge(s_ev, 3 * UT * NT)
                for c in range(KC):
                    ins = pe.matmul(ps[:, 2 + k, :], turned[:, k, c * P:(c + 1) * P], w[:, c, :],
                                    start=(c == 0), stop=(c == KC - 1))
                ins.then_inc(s_done, 1)

            def token_tiles(src, turned, bank, w, s_in, s_turned, s_copied, s_freed, s_done):
                in_pairs(pe, TT, lambda j, k: turn(j, k, src, bank, s_in, s_turned),
                         lambda j, k: product(j, k, turned, w, s_copied, s_freed, s_done), lag=1)

            token_tiles(tok_n, tok_t, 0, w1at, s_tn, s_tt, s_tc, s_tb, s_ta)
            pe.wait_ge(s_tc, TT)
            turn_weights(KC, KC + FC)
            pe.wait_ge(s_wc, KC + FC)
            pe.wait_ge(s_zf, 3)

            def turn_route(t, k):
                hold(pe, s_g[k], 16 * (t // 2 + 1), s_const)
                pe.transpose(ps[0:RANK, 6 + k, 0:P], route_a[:, k, :], ident[:]).then_inc(s_gt, 1)

            def up(t, k):
                wait(pe, s_gc, t + 1)
                wait(pe, s_wu[k], 16 * (t // 2 + 1))
                for b in range(4):
                    wait(pe, s_ge, 4 * (t - 1) + b + 1)
                    for f in range(FC // 4):
                        c = b * (FC // 4) + f
                        ins = pe.matmul(ps[:, b, f * P:(f + 1) * P], w1bs[:, k, c * P:(c + 1) * P],
                                        route_t[0:RANK, k, :], start=True, stop=True)
                    ins.then_inc(s_up, 1)

            def down(t, k):
                tt = t if isinstance(t, int) else pe.snap(t)
                e = pe.value_load(t_e[0:1, bass.ds(tt, 1)], min_val=0, max_val=E - 1)
                col = pe.snap(e * RANK)
                wait(pe, s_y, t - 1)
                for c in range(FC):
                    if c % (FC // 4) == 0:
                        wait(pe, s_ge, 4 * t + c // (FC // 4) + 1)
                    ins = pe.matmul(ps[:, 4 + k, 0:P], act_h[k][:, c, :], w2at[:, c, bass.ds(col, P)],
                                    start=(c == 0), stop=(c == FC - 1))
                ins.then_inc(s_dn, 1)

            turn_route(0, 0)
            up(0, 0)
            turn_route(1, 1)
            up(1, 1)
            turn_route(2, 0)
            down(0, 0)
            up(2, 0)
            turn_route(3, 1)
            down(1, 1)

            def route(t, k):
                up(t, k)
                turn_route(t + 1, 1 - k)
                down(t - 1, 1 - k)

            with pe.Fori(1, RT // 2 - 1) as q:
                route(q * 2 + 1, 1)
                route(q * 2 + 2, 0)
            up(RT - 1, 1)
            down(RT - 2, 0)
            down(RT - 1, 1)
            pe.wait_ge(s_y, RT)
            over_blocks(pe, 1, steps)
            between(NB - 1, 1)

            pe.wait_ge(s_wl, 16 * (2 + KC))
            token_tiles(res_n, res_t, 6, w2bs, s_rw, s_r1, s_r2, s_r4, s_r3)


_INS = ["L0_attn_x", "L0_attn_delta", "L0_attn_alpha", "L0_attn_beta", "L0_attn_gamma", "L0_attn_omega",
        "L0_ffn_expert_weights", "L0_ffn_expert_indices", "L0_ffn_w1_A", "L0_ffn_w1_B", "L0_ffn_w2_A",
        "L0_ffn_w2_B"]


def kernel(**inputs):
    import numpy as _np
    import concourse.bacc as _bacc
    from concourse import mybir as _mybir
    from concourse.bass_utils import run_bass_kernel_spmd as _run

    nc = _bacc.Bacc("TRN2", target_bir_lowering=False, num_devices=1)
    arrays, args = {}, []
    for name in _INS:
        a = _np.ascontiguousarray(inputs[name])
        arrays[name] = a
        args.append(nc.dram_tensor(name, a.shape, _mybir.dt.from_np(a.dtype), kind="ExternalInput").ap())
    shape = inputs["L0_attn_x"].shape
    args.append(nc.dram_tensor("out", shape, F32, kind="ExternalOutput").ap())
    build(nc, *args)
    r = _run(nc, [arrays], core_ids=[0])
    return r.results[0]["out"]
```
